# Optimizing a Trainium2 kernel written in Bass

```python
import numpy as np
import jax
import jax.numpy as jnp

def _softmax(x, axis=-1):
    return jax.nn.softmax(x, axis=axis)

def _gelu(x):
    return jax.nn.gelu(x, approximate=True)

def _silu(x):
    return jax.nn.silu(x)

def _sigmoid(x):
    return jax.nn.sigmoid(x)

def _layernorm(x, axis=-1, eps=1e-05):
    m = jnp.mean(x, axis=axis, keepdims=True)
    v = jnp.var(x, axis=axis, keepdims=True)
    return (x - m) / jnp.sqrt(v + eps)

def _scatter_add(tgt, idx, src, axis=0):
    return tgt.at[idx].add(src)

def _segment_sum(src, seg, n):
    return jax.ops.segment_sum(src, seg, n)
kernel_name = 'mk_hybrid_d1_jaxref_r8_a54e73'

def setup_inputs(seed: int=0):
    np.random.seed(seed)
    _w = jnp.asarray

    def _L0_attn_a_setup():
        import jax, jax.numpy as jnp
        import numpy as np
        from functools import partial
        B, S, D, H, DK, DV, DFF = (4, 256, 128, 8, 128, 128, 512)
        EPS = 1e-06

        def rms_norm(x):
            return x * jax.lax.rsqrt(jnp.mean(x * x, axis=-1, keepdims=True) + EPS)

        def l2norm(x):
            return x * jax.lax.rsqrt(jnp.sum(x * x, axis=-1, keepdims=True) + EPS)

        def gated_delta_net(h, Wq, Wk, Wv, Wb, Wa, A_log, dt_bias, Wg, o_norm_w, Wo):
            b, s, _ = h.shape
            q = l2norm(jax.nn.silu(h @ Wq).reshape(b, s, H, DK))
            k = l2norm(jax.nn.silu(h @ Wk).reshape(b, s, H, DK))
            v = jax.nn.silu(h @ Wv).reshape(b, s, H, DV)
            beta = jax.nn.sigmoid(h @ Wb)
            g = -jnp.exp(A_log) * jax.nn.softplus(h @ Wa + dt_bias)
            alpha = jnp.exp(g)
            scale = DK ** (-0.5)
            tm = lambda a: jnp.moveaxis(a, 1, 0)
            qs, ks_, vs, als, bts = (tm(q), tm(k), tm(v), tm(alpha), tm(beta))

            def step(Sst, inp):
                q_t, k_t, v_t, a_t, b_t = inp
                Sst = Sst * a_t[..., None, None]
                kv = jnp.einsum('bhd,bhde->bhe', k_t, Sst)
                delta = (v_t - kv) * b_t[..., None]
                Sst = Sst + jnp.einsum('bhd,bhe->bhde', k_t, delta)
                o_t = jnp.einsum('bhd,bhde->bhe', q_t, Sst) * scale
                return (Sst, o_t)
            S0 = jnp.zeros((b, H, DK, DV), dtype=h.dtype)
            _, o = jax.lax.scan(step, S0, (qs, ks_, vs, als, bts))
            o = jnp.moveaxis(o, 0, 1)
            gate = (h @ Wg).reshape(b, s, H, DV)
            o = rms_norm(o) * o_norm_w * jax.nn.silu(gate)
            return o.reshape(b, s, H * DV) @ Wo
        key = jax.random.key(seed)
        ks = jax.random.split(key, 16)
        w = lambda k, shp: jax.random.normal(k, shp, dtype=jnp.float32) * 0.02
        return {'x': jax.random.normal(ks[0], (B, S, D), dtype=jnp.float32), 'Wq': w(ks[1], (D, H * DK)), 'Wk': w(ks[2], (D, H * DK)), 'Wv': w(ks[3], (D, H * DV)), 'Wb': w(ks[4], (D, H)), 'Wa': w(ks[5], (D, H)), 'A_log': jnp.log(jnp.linspace(1.0, 8.0, H).astype(jnp.float32)), 'dt_bias': jax.random.normal(ks[6], (H,), dtype=jnp.float32) * 0.1, 'Wg': w(ks[7], (D, H * DV)), 'o_norm_w': jnp.ones((DV,), dtype=jnp.float32), 'Wo': w(ks[8], (H * DV, D)), 'W_fc': w(ks[9], (D, DFF)), 'W_proj': w(ks[10], (DFF, D))}
    _L0_attn_a_in = _L0_attn_a_setup()

    def _L0_attn_b_setup():
        import jax, jax.numpy as jnp
        import numpy as np
        B, T, D = (8, 256, 128)
        FF = 4 * D
        EPS = 1e-05

        def layer_norm(x, g, b):
            mu = jnp.mean(x, axis=-1, keepdims=True)
            var = jnp.var(x, axis=-1, keepdims=True)
            return (x - mu) * jax.lax.rsqrt(var + EPS) * g + b

        def token_shift(x):
            return jnp.pad(x, ((0, 0), (1, 0), (0, 0)))[:, :-1]

        def wkv_scan(k, v, time_decay, time_first):
            w = -jnp.exp(time_decay)
            u = time_first

            def step(carry, kv):
                aa, bb, pp = carry
                kt, vt = kv
                ww = u + kt
                p = jnp.maximum(pp, ww)
                e1 = jnp.exp(pp - p)
                e2 = jnp.exp(ww - p)
                out = (e1 * aa + e2 * vt) / (e1 * bb + e2)
                ww2 = pp + w
                p2 = jnp.maximum(ww2, kt)
                e1b = jnp.exp(ww2 - p2)
                e2b = jnp.exp(kt - p2)
                return ((e1b * aa + e2b * vt, e1b * bb + e2b, p2), out)
            z = jnp.zeros((k.shape[0], k.shape[2]), k.dtype)
            init = (z, z, jnp.full_like(z, -1e+38))
            _, outs = jax.lax.scan(step, init, (jnp.moveaxis(k, 1, 0), jnp.moveaxis(v, 1, 0)))
            return jnp.moveaxis(outs, 0, 1)
        key = jax.random.key(seed)
        ks = jax.random.split(key, 20)
        rn = lambda k, s, sc=0.02: jax.random.normal(k, s, jnp.float32) * sc
        return {'x': jax.random.normal(ks[0], (B, T, D), jnp.float32), 'ln1_g': jnp.ones((D,), jnp.float32), 'ln1_b': jnp.zeros((D,), jnp.float32), 'ln2_g': jnp.ones((D,), jnp.float32), 'ln2_b': jnp.zeros((D,), jnp.float32), 'tm_mix_k': jax.random.uniform(ks[1], (D,), jnp.float32), 'tm_mix_v': jax.random.uniform(ks[2], (D,), jnp.float32), 'tm_mix_r': jax.random.uniform(ks[3], (D,), jnp.float32), 'time_decay': rn(ks[4], (D,), 1.0), 'time_first': rn(ks[5], (D,), 0.5), 'wk': rn(ks[6], (D, D)), 'wv': rn(ks[7], (D, D)), 'wr': rn(ks[8], (D, D)), 'wo': rn(ks[9], (D, D)), 'cm_mix_k': jax.random.uniform(ks[10], (D,), jnp.float32), 'cm_mix_r': jax.random.uniform(ks[11], (D,), jnp.float32), 'cwk': rn(ks[12], (D, FF)), 'cwv': rn(ks[13], (FF, D)), 'cwr': rn(ks[14], (D, D))}
    _L0_attn_b_in = _L0_attn_b_setup()

    def _L0_ffn_setup():
        import jax, jax.numpy as jnp
        import numpy as np
        B, L, H, E, FF, C = (4, 256, 128, 8, 512, 2)
        key = jax.random.key(seed)
        ks = jax.random.split(key, 6)
        s = 0.02
        return {'x': jax.random.normal(ks[0], (B, L, H), dtype=jnp.float32), 'Wg': jax.random.normal(ks[1], (H, E), dtype=jnp.float32) * s, 'W1': jax.random.normal(ks[2], (E, H, FF), dtype=jnp.float32) * s, 'b1': jnp.zeros((E, FF), dtype=jnp.float32), 'W2': jax.random.normal(ks[3], (E, FF, H), dtype=jnp.float32) * s, 'b2': jnp.zeros((E, H), dtype=jnp.float32)}
    _L0_ffn_in = _L0_ffn_setup()
    _d = {'L0_attn_a_x': _L0_attn_a_in['x'], 'L0_attn_a_Wq': _L0_attn_a_in['Wq'], 'L0_attn_a_Wk': _L0_attn_a_in['Wk'], 'L0_attn_a_Wv': _L0_attn_a_in['Wv'], 'L0_attn_a_Wb': _L0_attn_a_in['Wb'], 'L0_attn_a_Wa': _L0_attn_a_in['Wa'], 'L0_attn_a_A_log': _L0_attn_a_in['A_log'], 'L0_attn_a_dt_bias': _L0_attn_a_in['dt_bias'], 'L0_attn_a_Wg': _L0_attn_a_in['Wg'], 'L0_attn_a_o_norm_w': _L0_attn_a_in['o_norm_w'], 'L0_attn_a_Wo': _L0_attn_a_in['Wo'], 'L0_attn_a_W_fc': _L0_attn_a_in['W_fc'], 'L0_attn_a_W_proj': _L0_attn_a_in['W_proj'], 'L0_attn_b_ln1_g': _L0_attn_b_in['ln1_g'], 'L0_attn_b_ln1_b': _L0_attn_b_in['ln1_b'], 'L0_attn_b_ln2_g': _L0_attn_b_in['ln2_g'], 'L0_attn_b_ln2_b': _L0_attn_b_in['ln2_b'], 'L0_attn_b_tm_mix_k': _L0_attn_b_in['tm_mix_k'], 'L0_attn_b_tm_mix_v': _L0_attn_b_in['tm_mix_v'], 'L0_attn_b_tm_mix_r': _L0_attn_b_in['tm_mix_r'], 'L0_attn_b_time_decay': _L0_attn_b_in['time_decay'], 'L0_attn_b_time_first': _L0_attn_b_in['time_first'], 'L0_attn_b_wk': _L0_attn_b_in['wk'], 'L0_attn_b_wv': _L0_attn_b_in['wv'], 'L0_attn_b_wr': _L0_attn_b_in['wr'], 'L0_attn_b_wo': _L0_attn_b_in['wo'], 'L0_attn_b_cm_mix_k': _L0_attn_b_in['cm_mix_k'], 'L0_attn_b_cm_mix_r': _L0_attn_b_in['cm_mix_r'], 'L0_attn_b_cwk': _L0_attn_b_in['cwk'], 'L0_attn_b_cwv': _L0_attn_b_in['cwv'], 'L0_attn_b_cwr': _L0_attn_b_in['cwr'], 'L0_ffn_Wg': _L0_ffn_in['Wg'], 'L0_ffn_W1': _L0_ffn_in['W1'], 'L0_ffn_b1': _L0_ffn_in['b1'], 'L0_ffn_W2': _L0_ffn_in['W2'], 'L0_ffn_b2': _L0_ffn_in['b2']}
    _x0 = _d['L0_attn_a_x']
    _d['L0_attn_a_x'] = jax.random.normal(jax.random.fold_in(jax.random.key(seed), 1), (16, 512, 128), dtype=_x0.dtype)
    del _x0
    return _d

def reference(L0_attn_a_x, L0_attn_a_Wq, L0_attn_a_Wk, L0_attn_a_Wv, L0_attn_a_Wb, L0_attn_a_Wa, L0_attn_a_A_log, L0_attn_a_dt_bias, L0_attn_a_Wg, L0_attn_a_o_norm_w, L0_attn_a_Wo, L0_attn_a_W_fc, L0_attn_a_W_proj, L0_attn_b_ln1_g, L0_attn_b_ln1_b, L0_attn_b_ln2_g, L0_attn_b_ln2_b, L0_attn_b_tm_mix_k, L0_attn_b_tm_mix_v, L0_attn_b_tm_mix_r, L0_attn_b_time_decay, L0_attn_b_time_first, L0_attn_b_wk, L0_attn_b_wv, L0_attn_b_wr, L0_attn_b_wo, L0_attn_b_cm_mix_k, L0_attn_b_cm_mix_r, L0_attn_b_cwk, L0_attn_b_cwv, L0_attn_b_cwr, L0_ffn_Wg, L0_ffn_W1, L0_ffn_b1, L0_ffn_W2, L0_ffn_b2):

    def _L0_attn_a_ref(x, Wq, Wk, Wv, Wb, Wa, A_log, dt_bias, Wg, o_norm_w, Wo, W_fc, W_proj):
        import jax, jax.numpy as jnp
        import numpy as np
        from functools import partial
        B, S, D, H, DK, DV, DFF = (4, 256, 128, 8, 128, 128, 512)
        EPS = 1e-06

        def rms_norm(x):
            return x * jax.lax.rsqrt(jnp.mean(x * x, axis=-1, keepdims=True) + EPS)

        def l2norm(x):
            return x * jax.lax.rsqrt(jnp.sum(x * x, axis=-1, keepdims=True) + EPS)

        def gated_delta_net(h, Wq, Wk, Wv, Wb, Wa, A_log, dt_bias, Wg, o_norm_w, Wo):
            b, s, _ = h.shape
            q = l2norm(jax.nn.silu(h @ Wq).reshape(b, s, H, DK))
            k = l2norm(jax.nn.silu(h @ Wk).reshape(b, s, H, DK))
            v = jax.nn.silu(h @ Wv).reshape(b, s, H, DV)
            beta = jax.nn.sigmoid(h @ Wb)
            g = -jnp.exp(A_log) * jax.nn.softplus(h @ Wa + dt_bias)
            alpha = jnp.exp(g)
            scale = DK ** (-0.5)
            tm = lambda a: jnp.moveaxis(a, 1, 0)
            qs, ks_, vs, als, bts = (tm(q), tm(k), tm(v), tm(alpha), tm(beta))

            def step(Sst, inp):
                q_t, k_t, v_t, a_t, b_t = inp
                Sst = Sst * a_t[..., None, None]
                kv = jnp.einsum('bhd,bhde->bhe', k_t, Sst)
                delta = (v_t - kv) * b_t[..., None]
                Sst = Sst + jnp.einsum('bhd,bhe->bhde', k_t, delta)
                o_t = jnp.einsum('bhd,bhde->bhe', q_t, Sst) * scale
                return (Sst, o_t)
            S0 = jnp.zeros((b, H, DK, DV), dtype=h.dtype)
            _, o = jax.lax.scan(step, S0, (qs, ks_, vs, als, bts))
            o = jnp.moveaxis(o, 0, 1)
            gate = (h @ Wg).reshape(b, s, H, DV)
            o = rms_norm(o) * o_norm_w * jax.nn.silu(gate)
            return o.reshape(b, s, H * DV) @ Wo
        ln_scale = 1.0
        h = gated_delta_net(ln_scale * rms_norm(x), Wq, Wk, Wv, Wb, Wa, A_log, dt_bias, Wg, o_norm_w, Wo)
        x = x + h
        m = ln_scale * rms_norm(x)
        y = jnp.square(jax.nn.relu(m @ W_fc)) @ W_proj
        return x + y

    def _L0_attn_b_ref(x, ln1_g, ln1_b, ln2_g, ln2_b, tm_mix_k, tm_mix_v, tm_mix_r, time_decay, time_first, wk, wv, wr, wo, cm_mix_k, cm_mix_r, cwk, cwv, cwr):
        import jax, jax.numpy as jnp
        import numpy as np
        B, T, D = (8, 256, 128)
        FF = 4 * D
        EPS = 1e-05

        def layer_norm(x, g, b):
            mu = jnp.mean(x, axis=-1, keepdims=True)
            var = jnp.var(x, axis=-1, keepdims=True)
            return (x - mu) * jax.lax.rsqrt(var + EPS) * g + b

        def token_shift(x):
            return jnp.pad(x, ((0, 0), (1, 0), (0, 0)))[:, :-1]

        def wkv_scan(k, v, time_decay, time_first):
            w = -jnp.exp(time_decay)
            u = time_first

            def step(carry, kv):
                aa, bb, pp = carry
                kt, vt = kv
                ww = u + kt
                p = jnp.maximum(pp, ww)
                e1 = jnp.exp(pp - p)
                e2 = jnp.exp(ww - p)
                out = (e1 * aa + e2 * vt) / (e1 * bb + e2)
                ww2 = pp + w
                p2 = jnp.maximum(ww2, kt)
                e1b = jnp.exp(ww2 - p2)
                e2b = jnp.exp(kt - p2)
                return ((e1b * aa + e2b * vt, e1b * bb + e2b, p2), out)
            z = jnp.zeros((k.shape[0], k.shape[2]), k.dtype)
            init = (z, z, jnp.full_like(z, -1e+38))
            _, outs = jax.lax.scan(step, init, (jnp.moveaxis(k, 1, 0), jnp.moveaxis(v, 1, 0)))
            return jnp.moveaxis(outs, 0, 1)
        h = layer_norm(x, ln1_g, ln1_b)
        hx = token_shift(h)
        k = jnp.einsum('btd,de->bte', h * tm_mix_k + hx * (1.0 - tm_mix_k), wk)
        v = jnp.einsum('btd,de->bte', h * tm_mix_v + hx * (1.0 - tm_mix_v), wv)
        r = jax.nn.sigmoid(jnp.einsum('btd,de->bte', h * tm_mix_r + hx * (1.0 - tm_mix_r), wr))
        wkv = wkv_scan(k, v, time_decay, time_first)
        x = x + jnp.einsum('btd,de->bte', r * wkv, wo)
        h = layer_norm(x, ln2_g, ln2_b)
        hx = token_shift(h)
        kk = jnp.einsum('btd,df->btf', h * cm_mix_k + hx * (1.0 - cm_mix_k), cwk)
        kk = jnp.square(jax.nn.relu(kk))
        rr = jax.nn.sigmoid(jnp.einsum('btd,de->bte', h * cm_mix_r + hx * (1.0 - cm_mix_r), cwr))
        x = x + rr * jnp.einsum('btf,fd->btd', kk, cwv)
        return x

    def _L0_ffn_ref(x, Wg, W1, b1, W2, b2):
        import jax, jax.numpy as jnp
        import numpy as np
        B, L, H, E, FF, C = (4, 256, 128, 8, 512, 2)
        b, l, h = x.shape
        e = Wg.shape[1]
        n = b * l
        k = min(max(int(n * C / e), 1), n)
        xt = x.reshape(n, h)
        S = jax.nn.sigmoid(xt @ Wg).T
        G, I = jax.lax.top_k(S, k)
        ex = xt[I]
        hid = jax.nn.gelu(jnp.einsum('ekh,ehf->ekf', ex, W1) + b1[:, None, :], approximate=False)
        out = (jnp.einsum('ekf,efh->ekh', hid, W2) + b2[:, None, :]) * G[..., None]
        new_x = jnp.zeros_like(xt).at[I.reshape(-1)].add(out.reshape(-1, h))
        return new_x.reshape(b, l, h)
    x = L0_attn_a_x
    x = x + _L0_attn_a_ref(_layernorm(x, axis=-1), L0_attn_a_Wq, L0_attn_a_Wk, L0_attn_a_Wv, L0_attn_a_Wb, L0_attn_a_Wa, L0_attn_a_A_log, L0_attn_a_dt_bias, L0_attn_a_Wg, L0_attn_a_o_norm_w, L0_attn_a_Wo, L0_attn_a_W_fc, L0_attn_a_W_proj)
    x = x + _L0_ffn_ref(_layernorm(x, axis=-1), L0_ffn_Wg, L0_ffn_W1, L0_ffn_b1, L0_ffn_W2, L0_ffn_b2)
    x = x + _L0_attn_b_ref(_layernorm(x, axis=-1), L0_attn_b_ln1_g, L0_attn_b_ln1_b, L0_attn_b_ln2_g, L0_attn_b_ln2_b, L0_attn_b_tm_mix_k, L0_attn_b_tm_mix_v, L0_attn_b_tm_mix_r, L0_attn_b_time_decay, L0_attn_b_time_first, L0_attn_b_wk, L0_attn_b_wv, L0_attn_b_wr, L0_attn_b_wo, L0_attn_b_cm_mix_k, L0_attn_b_cm_mix_r, L0_attn_b_cwk, L0_attn_b_cwv, L0_attn_b_cwr)
    x = x + _L0_ffn_ref(_layernorm(x, axis=-1), L0_ffn_Wg, L0_ffn_W1, L0_ffn_b1, L0_ffn_W2, L0_ffn_b2)
    return x

_drawn_inputs = setup_inputs


def setup_inputs(seed=0):
    import zlib

    import numpy as np

    out = dict(_drawn_inputs(seed))
    spreads = {'L0_attn_a_o_norm_w': (1.0, 0.6),
     'L0_attn_b_ln1_g': (1.0, 0.6),
     'L0_attn_b_ln1_b': (0.0, 0.8),
     'L0_attn_b_ln2_g': (1.0, 0.6),
     'L0_attn_b_ln2_b': (0.0, 0.8),
     'L0_ffn_b1': (0.0, 0.497),
     'L0_ffn_b2': (0.0, 0.1)}
    factors = {'L0_attn_a_Wq': 3.681,
     'L0_attn_a_Wk': 3.681,
     'L0_attn_a_Wv': 3.668,
     'L0_attn_a_Wb': 8.0,
     'L0_attn_a_Wa': 8.0,
     'L0_attn_a_A_log': 8.0,
     'L0_attn_a_dt_bias': 8.0,
     'L0_attn_a_Wg': 3.664,
     'L0_attn_a_Wo': 3.659,
     'L0_attn_a_W_fc': 4.04,
     'L0_attn_a_W_proj': 3.774,
     'L0_attn_b_tm_mix_k': 8.0,
     'L0_attn_b_tm_mix_v': 8.0,
     'L0_attn_b_tm_mix_r': 8.0,
     'L0_attn_b_time_decay': 8.0,
     'L0_attn_b_time_first': 8.0,
     'L0_attn_b_wk': 8.0,
     'L0_attn_b_wv': 8.0,
     'L0_attn_b_wr': 8.0,
     'L0_attn_b_wo': 8.0,
     'L0_attn_b_cm_mix_k': 8.0,
     'L0_attn_b_cm_mix_r': 8.0,
     'L0_attn_b_cwk': 8.0,
     'L0_attn_b_cwv': 8.0,
     'L0_attn_b_cwr': 8.0}
    for name, (base, spread) in spreads.items():
        noise = np.random.default_rng([zlib.crc32(name.encode()), seed]).standard_normal(out[name].shape)
        drawn = base * np.exp(spread * noise) if base else spread * noise
        out[name] = jnp.asarray(drawn.astype(out[name].dtype))
    for name, factor in factors.items():
        out[name] = (out[name] * factor).astype(out[name].dtype)
    return out
```

```python
import numpy as np
import concourse.bass as bass
from concourse import mybir
from contextlib import ExitStack

F32 = mybir.dt.float32
I32 = mybir.dt.int32
ALU = mybir.AluOpType
ACT = mybir.ActivationFunctionType
AX = mybir.AxisListType

P = 128
B, S, D = 16, 512, 128
NT = B * S // P
TPB = S // P
H, DK = 8, 128
HG = 4
NG = H // HG
FF = 512
NF = FF // P
E = 8
CAP = 2 * B * S // E
SEG = E * B // P * S
LEVELS = 7
BITS = 30


def bc(ap, n):
    return ap.unsqueeze(2).to_broadcast([ap.shape[0], ap.shape[1], n])


class Space:

    def __init__(self, nc, tag):
        self.nc, self.tag, self.ctx, self.sems = nc, tag, ExitStack(), []

    def __enter__(self):
        self.ctx.__enter__()
        return self

    def __exit__(self, *a):
        self.ctx.__exit__(*a)
        if self.sems:
            self.nc.clear_and_free_semaphores(self.sems)
            self.nc.all_engine_barrier()

    def sb(self, name, shape, dt=F32):
        return self.ctx.enter_context(self.nc.sbuf_tensor(f"{self.tag}_{name}", shape, dt))

    def ps(self, name, shape=(P, 512)):
        return self.ctx.enter_context(self.nc.psum_tensor(f"{self.tag}_{name}", list(shape), F32))

    def sem(self, name):
        self.sems.append(self.nc.alloc_semaphore(f"{self.tag}_{name}"))
        return self.sems[-1]

    def block(self):
        return self.ctx.enter_context(self.nc.Block())


def load_phase(nc, M, I, tag):
    with Space(nc, tag) as s:
        loaded = s.sem("loaded")
        padded = s.sem("padded")
        block = s.block()

        @block.sync
        def _(sp):
            sp.dma_start(M.X[:, :, :], I["x"].rearrange("b (t p) d -> p (b t) d", p=P)).then_inc(loaded, 16)
            sp.wait_ge(loaded, 16)

        @block.scalar
        def _(act):
            act.dma_start(M.ident[:, :], I["ident"]).then_inc(padded, 16)
            act.wait_ge(padded, 16)

        @block.vector
        def _(dve):
            nc.vector.memset(M.HT[:, :, 0:1], 0.0)


def norm_phase(nc, M, tag, src, eps, eps2=None, rms=False, keep=None, affine=None):
    with Space(nc, tag) as s:
        stats = s.sb("stats", [P, NT, 6])
        mean = s.sb("mean", [P, NT])
        var = s.sb("var", [P, NT])
        tmp = s.sb("tmp", [P, NT])
        root = s.sb("root", [P, NT])
        s1 = s.sb("s1", [P, NT])
        s12 = s.sb("s12", [P, NT])
        shift = s.sb("shift", [P, NT])
        stage = [s.sb(f"stage{p}", [P, TPB, D]) for p in range(2)]
        turned = [s.ps(f"turned{p}") for p in range(2)]
        stats_ready = s.sem("stats_ready")
        var_ready = s.sem("var_ready")
        root_ready = s.sem("root_ready")
        chain = s.sem("chain")
        scale_ready = s.sem("scale_ready")
        staged = s.sem("staged")
        turned_ready = s.sem("turned_ready")
        copied = s.sem("copied")
        kept = s.sem("kept")
        block = s.block()

        @block.vector
        def _(dve):
            links = [0]

            def link(ins):
                ins.then_inc(chain, 1)
                links[0] += 1
                dve.wait_ge(chain, links[0])

            with dve.Fori(0, B) as b:
                for j in range(TPB):
                    last = nc.vector.bn_stats(stats[:, bass.ds(b * TPB + j, 1), :].rearrange("p a s -> p (a s)"),
                                              src[:, bass.ds(b * TPB + j, 1), :].rearrange("p a d -> p (a d)"))
                last.then_inc(stats_ready, 1)
            dve.wait_ge(stats_ready, B)
            even, odd = stats[:, :, 0:3], stats[:, :, 3:6]
            link(nc.vector.tensor_tensor(mean[:, :], even[:, :, 1], odd[:, :, 1], ALU.add))
            link(nc.vector.tensor_scalar(mean[:, :], mean[:, :], 0.5, None, ALU.mult))
            link(nc.vector.tensor_tensor(tmp[:, :], even[:, :, 1], odd[:, :, 1], ALU.subtract))
            link(nc.vector.tensor_tensor(tmp[:, :], tmp[:, :], tmp[:, :], ALU.mult))
            link(nc.vector.tensor_tensor(var[:, :], even[:, :, 2], odd[:, :, 2], ALU.add))
            link(nc.vector.tensor_scalar(var[:, :], var[:, :], 1.0 / D, None, ALU.mult))
            link(nc.vector.scalar_tensor_tensor(var[:, :], tmp[:, :], 0.25, var[:, :], ALU.mult, ALU.add))
            if rms:
                link(nc.vector.tensor_tensor(tmp[:, :], mean[:, :], mean[:, :], ALU.mult))
                link(nc.vector.tensor_tensor(s1[:, :], tmp[:, :], var[:, :], ALU.add))
                nc.vector.tensor_scalar(tmp[:, :], s1[:, :], eps, None, ALU.add).then_inc(var_ready, 1)
            else:
                nc.vector.tensor_scalar(tmp[:, :], var[:, :], eps, None, ALU.add).then_inc(var_ready, 1)
            dve.wait_ge(root_ready, 1)
            link(nc.vector.reciprocal(s1[:, :], root[:, :]))
            if eps2 is not None:
                link(nc.vector.tensor_tensor(s12[:, :], s1[:, :], s1[:, :], ALU.mult))
                link(nc.vector.tensor_tensor(shift[:, :], s12[:, :], var[:, :], ALU.mult))
                nc.vector.tensor_scalar(tmp[:, :], shift[:, :], eps2, None, ALU.add).then_inc(var_ready, 1)
                dve.wait_ge(root_ready, 2)
                link(nc.vector.reciprocal(tmp[:, :], root[:, :]))
                link(nc.vector.tensor_tensor(s12[:, :], s1[:, :], tmp[:, :], ALU.mult))
            total = s1 if eps2 is None else s12
            if rms:
                link(nc.vector.memset(shift[:, :], 0.0))
                nc.vector.tensor_copy(s12[:, :], s1[:, :]).then_inc(scale_ready, 1)
            else:
                if eps2 is None:
                    link(nc.vector.tensor_copy(s12[:, :], s1[:, :]))
                nc.vector.scalar_tensor_tensor(shift[:, :], mean[:, :], -1.0, total[:, :], ALU.mult,
                                               ALU.mult).then_inc(scale_ready, 1)
            dve.sem_inc(copied, 2)
            with dve.Fori(0, B // 2) as i:
                for p in range(2):
                    if keep is not None:
                        for j in range(TPB):
                            t = (2 * i + p) * TPB + j
                            last = nc.vector.tensor_scalar(keep[:, bass.ds(t, 1), :], src[:, bass.ds(t, 1), :],
                                                           mean[:, bass.ds(t, 1)], s1[:, bass.ds(t, 1)],
                                                           ALU.subtract, ALU.mult)
                        last.then_inc(kept, 1)
                    out = M.HT[:, bass.ds(2 * i + p, 1), 1:1 + S].rearrange("p a n -> p (a n)")
                    dve.wait_ge(turned_ready, 2 * i + p + 3)
                    if affine is None:
                        nc.vector.tensor_copy(out, turned[p][:, :]).then_inc(copied, 1)
                    else:
                        nc.vector.tensor_scalar(out, turned[p][:, :], affine[0], affine[1], ALU.mult,
                                                ALU.add).then_inc(copied, 1)

        @block.scalar
        def _(act):
            for k in range(1 if eps2 is None else 2):
                act.wait_ge(var_ready, k + 1)
                nc.scalar.activation(root[:, :], tmp[:, :], ACT.Sqrt).then_inc(root_ready, 1)
            act.wait_ge(scale_ready, 1)
            with act.Fori(0, B // 2) as i:
                for p in range(2):
                    act.wait_ge(turned_ready, 2 * i + p + 1)
                    for j in range(TPB):
                        t = (2 * i + p) * TPB + j
                        last = nc.scalar.activation(stage[p][:, j, :], src[:, bass.ds(t, 1), :].rearrange("p a d -> p (a d)"),
                                                    ACT.Identity, bias=shift[:, bass.ds(t, 1)], scale=s12[:, bass.ds(t, 1)])
                    last.then_inc(staged, 1)

        @block.tensor
        def _(pe):
            pe.sem_inc(turned_ready, 2)
            with pe.Fori(0, B // 2) as i:
                for p in range(2):
                    pe.wait_ge(staged, 2 * i + p + 1)
                    pe.wait_ge(copied, 2 * i + p + 1)
                    for j in range(TPB):
                        last = nc.tensor.transpose(turned[p][:, j * P:(j + 1) * P], stage[p][:, j, :], M.ident[:, :])
                    last.then_inc(turned_ready, 1)

def gdn_gates(nc, M, I, T, alpha_dram):
    Q = NT * H // P
    with Space(nc, "gg") as s:
        wba = s.sb("wba", [P, 2 * H])
        a_rate = s.sb("a_rate", [P, 1])
        dt_bias = s.sb("dt_bias", [P, 1])
        out_now = [s.sb(f"out_now{p}", [2 * H, S]) for p in range(2)]
        zb = s.sb("zb", [P, Q, P])
        za = s.sb("za", [P, Q, P])
        small = s.sb("small", [P, Q * P])
        grown = s.sb("grown", [P, Q * P])
        log = s.sb("log", [P, Q * P])
        none = s.sb("none", [P, Q * P])
        g_row = s.sb("g_row", [P, Q, P])
        z_dram = nc.dram_tensor("gates_z_dram", [2, NT * H, P], F32, kind="Internal").ap()
        end_dram = nc.dram_tensor("gates_end_dram", [NT * H], F32, kind="Internal").ap()
        pz = [s.ps(f"pz{p}", [2 * H, S]) for p in range(2)]
        pt = [s.ps(f"pt{p}") for p in range(2)]
        (loaded, z_ready, z_copied, z_in, act_ready, chain, alpha_ready, g_ready, turned, table_ready, end_out, dram_out) = (
            s.sem(n) for n in ("loaded", "z_ready", "z_copied", "z_in", "act_ready", "chain", "alpha_ready",
                               "g_ready", "turned", "table_ready", "end_out", "dram_out"))
        z_out = [s.sem(f"z_out{p}") for p in range(2)]
        block = s.block()
        flat = lambda x: x[:, :, :].rearrange("p q n -> p (q n)")

        @block.sync
        def _(sp):
            sp.dma_start(wba[:, 0:H], I["Wb"]).then_inc(loaded, 16)
            sp.dma_start(wba[:, H:2 * H], I["Wa"]).then_inc(loaded, 16)
            sp.dma_start(a_rate[:, :], I["A_log_rows"]).then_inc(loaded, 16)
            sp.dma_start(dt_bias[:, :], I["dt_bias_rows"]).then_inc(loaded, 16)
            with sp.Fori(0, B // 2) as i:
                for p in range(2):
                    b = 2 * i + p
                    sp.wait_ge(z_copied, b + 3)
                    for n in range(2):
                        sp.dma_start(z_dram[n, bass.ds(b * TPB * H, TPB * H), :].rearrange("(t h) n -> h t n", h=H),
                                     out_now[p][n * H:(n + 1) * H, :].rearrange("h (t n) -> h t n", n=P)).then_inc(z_out[p], 16)
            for p in range(2):
                sp.wait_ge(z_out[p], 32 * (B // 2))
            sp.dma_start(zb[:, :, :], z_dram[0].rearrange("(q p) n -> p q n", p=P)).then_inc(z_in, 16)
            sp.dma_start(za[:, :, :], z_dram[1].rearrange("(q p) n -> p q n", p=P)).then_inc(z_in, 16)
            sp.wait_ge(table_ready, 1)
            sp.dma_start(end_dram.rearrange("(a n) -> a n", a=1), T.g[P - 1:P, :, :].rearrange("p t h -> p (t h)")).then_inc(end_out, 16)
            sp.wait_ge(end_out, 16)
            sp.dma_start(T.end[:, :, :].rearrange("p t h -> p (t h)"), end_dram.partition_broadcast(P)).then_inc(end_out, 16)
            sp.wait_ge(alpha_ready, 1)
            sp.dma_start(alpha_dram.rearrange("(q p) n -> p q n", p=P), za[:, :, :]).then_inc(dram_out, 16)
            sp.wait_ge(dram_out, 16)
            sp.wait_ge(end_out, 32)

        @block.tensor
        def _(pe):
            pe.wait_ge(loaded, 64)
            with pe.Fori(0, B // 2) as i:
                for p in range(2):
                    pe.wait_ge(z_copied, 2 * i + p + 1)
                    nc.tensor.matmul(pz[p][:, :], wba[:, :], M.HT[:, bass.ds(2 * i + p, 1), 1:1 + S].rearrange("p a n -> p (a n)"),
                                     start=True, stop=True).then_inc(z_ready, 1)
            pe.wait_ge(act_ready, 3)
            for q in range(Q):
                nc.tensor.transpose(pt[0][:, q * P:(q + 1) * P], zb[:, q, :], M.ident[:, :])
            pe.wait_ge(g_ready, 1)
            for q in range(Q):
                last = nc.tensor.transpose(pt[1][:, q * P:(q + 1) * P], g_row[:, q, :], M.ident[:, :])
            last.then_inc(turned, 1)

        @block.scalar
        def _(act):
            act.wait_ge(z_in, 32)
            nc.scalar.activation(a_rate[:, :], a_rate[:, :], ACT.Exp).then_inc(act_ready, 1)
            nc.scalar.activation(small[:, :], flat(za), ACT.Abs, bias=dt_bias[:, :]).then_inc(chain, 1)
            act.wait_ge(chain, 1)
            nc.scalar.activation(small[:, :], small[:, :], ACT.Exp, scale=-1.0).then_inc(act_ready, 1)
            nc.scalar.activation(flat(zb), flat(zb), ACT.Sigmoid).then_inc(act_ready, 1)
            act.wait_ge(chain, 2)
            nc.scalar.activation(log[:, :], grown[:, :], ACT.Ln).then_inc(act_ready, 1)
            act.wait_ge(alpha_ready, 1)
            nc.scalar.activation(flat(za), log[:, :], ACT.Exp).then_inc(act_ready, 1)

        @block.vector
        def _(dve):
            links = [1]

            def link(ins):
                ins.then_inc(chain, 1)
                links[0] += 1
                dve.wait_ge(chain, links[0])

            dve.sem_inc(z_copied, 2)
            with dve.Fori(0, B // 2) as i:
                for p in range(2):
                    dve.wait_ge(z_ready, 2 * i + p + 1)
                    dve.wait_ge(z_out[p], 32 * i)
                    nc.vector.tensor_copy(out_now[p][:, :], pz[p][:, :]).then_inc(z_copied, 1)
            dve.wait_ge(act_ready, 2)
            link(nc.vector.tensor_scalar(grown[:, :], small[:, :], 1.0, None, ALU.add))
            dve.wait_ge(act_ready, 4)
            link(nc.vector.tensor_scalar(none[:, :], grown[:, :], 1.0, None, ALU.is_equal))
            link(nc.vector.scalar_tensor_tensor(grown[:, :], grown[:, :], -1.0, none[:, :], ALU.add, ALU.add))
            link(nc.vector.tensor_tensor(log[:, :], log[:, :], none[:, :], ALU.add))
            link(nc.vector.reciprocal(none[:, :], grown[:, :]))
            link(nc.vector.tensor_tensor(log[:, :], log[:, :], none[:, :], ALU.mult))
            link(nc.vector.tensor_tensor(log[:, :], log[:, :], small[:, :], ALU.mult))
            link(nc.vector.tensor_scalar(flat(za), flat(za), dt_bias[:, :], 0.0, ALU.add, ALU.max))
            link(nc.vector.tensor_tensor(log[:, :], log[:, :], flat(za), ALU.add))
            nc.vector.tensor_scalar(log[:, :], log[:, :], a_rate[:, :], -1.0, ALU.mult, ALU.mult).then_inc(alpha_ready, 1)
            dve.wait_ge(act_ready, 5)
            for q in range(Q):
                last = nc.vector.tensor_tensor_scan(g_row[:, q, :], za[:, q, :], za[:, q, :], 1.0, ALU.mult, ALU.bypass)
            last.then_inc(g_ready, 1)
            dve.wait_ge(g_ready, 1)
            nc.vector.memset(za[:, :, 0:1], 0.0).then_inc(alpha_ready, 1)
            dve.wait_ge(turned, 1)
            fl = lambda x: x[:, :, :].rearrange("p t h -> p (t h)")
            nc.vector.tensor_copy(fl(T.beta), pt[0][:, :])
            nc.vector.tensor_scalar(fl(T.minus_beta), pt[0][:, :], -1.0, None, ALU.mult)
            nc.vector.tensor_copy(fl(T.g), pt[1][:, :]).then_inc(table_ready, 1)


def gdn_phase(nc, M, I):
    alpha_dram = nc.dram_tensor("alpha_dram", [NT * H, P], F32, kind="Internal").ap()
    with Space(nc, "gt") as tb:
        class T:
            beta = tb.sb("beta", [P, NT, H])
            minus_beta = tb.sb("minus_beta", [P, NT, H])
            g = tb.sb("g", [P, NT, H])
            end = tb.sb("end", [P, NT, H])
        gdn_gates(nc, M, I, T, alpha_dram)
        gdn_main(nc, M, I, T, alpha_dram)


def gdn_main(nc, M, I, T, alpha_dram):
    with Space(nc, "gd") as s:
        w_all = s.sb("w_all", [P, 4, H * DK])
        wo = s.sb("wo", [P, H, D])
        o_norm = s.sb("o_norm", [P, 1])
        mask_w = s.sb("mask_w", [P, LEVELS, P], I32)
        mask_t = s.sb("mask_t", [P, LEVELS, P], I32)
        four_ident = s.sb("four_ident", [P, HG, P])
        eps_q = s.sb("eps_q", [P, 1])
        eps_1 = s.sb("eps_1", [P, 1])
        ht = s.sb("ht", [P, P])
        alpha = s.sb("alpha", [P, H * P])
        group = lambda name: [s.sb(f"{name}{g}", [P, HG, P]) for g in range(NG)]
        (q_s, v_s, q_t, k_t, decay, decay_b, neg_lt, attn_t, inv, inv_t, y_s, state, state_g, rhs,
         delta, delta_d, o, sq_q, sq_k, o_t) = (group(n) for n in (
             "q_s", "v_s", "q_t", "k_t", "decay", "decay_b", "neg_lt", "attn_t", "inv", "inv_t",
             "y_s", "state", "state_g", "rhs", "delta", "delta_d", "o", "sq_q", "sq_k", "o_t"))
        k_s, z_s = ([group(f"{n}{par}_") for par in range(2)] for n in ("k_s", "z_s"))
        end_decay = [s.sb(f"end_decay{par}", [P, NG, HG]) for par in range(2)]
        sum_sq, root, unit = (s.sb(n, [P, NG, 2, HG]) for n in ("sum_sq", "root", "unit"))
        o_sum, o_root, o_unit = (s.sb(n, [P, NG, HG]) for n in ("o_sum", "o_root", "o_unit"))
        LV = range(1, LEVELS)

        uses = {}
        for g in range(NG):
            uses[f"Y{g}"] = [(c, u) for c in range(TPB) for u in [f"Y{l}" for l in LV] + ["E", "PD", "o_t"]
                             + (["out"] if g == 0 else [])]
            uses[f"Z{g}"] = [(c, u) for c in range(TPB) for u in ["L0"] + (["KS", "QS"] if c else [])
                             + [f"Z{l}" for l in LV] + ["dS"]]
        for name, first, then in (("q", "q", "k_t"), ("k", "k", "q_t"), ("v", "v", "KK"), ("z", "z", "KQ")):
            uses[name] = [(c, f"{u}{g}") for c in range(TPB) for u in (first, then) for g in range(NG)]
        bank = {n: s.ps(n) for n in uses}
        filled = {n: s.sem(f"filled_{n}") for n in uses}
        drained = {n: s.sem(f"drained_{n}") for n in uses}
        made = {n: s.sem(n) for n in ("ht_copied", "squares", "sums", "roots", "units", "k_unit", "q_unit", "inv_init",
                                      "state_decayed", "scanned", "decay_beta", "w_grown", "w_t0", "rhs_ready",
                                      "delta_decayed", "o_squares", "o_sums", "o_roots", "o_units",
                                      "o_gated", "o_normed")}
        loaded, prepared, alpha_in, wait_taken, copy_wait_taken = (
            s.sem(n) for n in ("loaded", "prepared", "alpha_in", "wait_taken", "copy_wait_taken"))
        block = s.block()
        flat = lambda x: x[:, :, :].rearrange("p h n -> p (h n)")
        hs = lambda g: slice(g * HG, (g + 1) * HG)
        LOW, HIGH = 0, 1

        def half(x, l, which):
            return x.rearrange("p h (a two s) -> p h a two s", two=2, s=1 << l)[:, :, :, which, :]

        def packed(ps, l):
            return ps.rearrange("p (h a s) -> p h a s", h=HG, s=1 << l)

        def wait_full(eng, name, use, b, c):
            eng.wait_ge(filled[name], len(uses[name]) * b + uses[name].index((c, use)) + 1)

        def wait_drained(eng, name, use, b, c):
            eng.wait_ge(drained[name], len(uses[name]) * b + uses[name].index((c, use)) + 1)

        def wait_free(eng, name, use, b, c):
            eng.wait_ge(drained[name], len(uses[name]) * b + uses[name].index((c, use)))

        def wait_made(eng, name, b, c, g):
            if name in ("rhs_ready", "state_decayed"):
                assert c > 0
                eng.wait_ge(made[name], NG * (TPB - 1) * b + NG * (c - 1) + g + 1)
            else:
                eng.wait_ge(made[name], NG * (TPB * b + c) + g + 1)

        def wait_grown(eng, b, c, l, g):
            eng.wait_ge(made["w_grown"], NG * (LEVELS - 1) * (TPB * b + c) + NG * l + g + 1)

        def before(b, c):
            if c:
                return b, c - 1
            return None if isinstance(b, int) and b == 0 else (b - 1, TPB - 1)

        def per_token(table, b, c, g):
            return table[:, bass.ds(b * TPB + c, 1), hs(g)].rearrange("p a h -> p (a h)")

        def schedule(eng, front, back):
            front(0, 0)
            with eng.Fori(0, B - 1) as b:
                for c in range(TPB):
                    back(b, c, (b, c + 1) if c + 1 < TPB else (b + 1, 0))
            for c in range(TPB):
                back(B - 1, c, (B - 1, c + 1) if c + 1 < TPB else None)

        @block.sync
        def _(sp):
            for n, name in enumerate(("Wq", "Wk", "Wv", "Wg")):
                sp.dma_start(w_all[:, n, :], I[name]).then_inc(loaded, 16)
            sp.dma_start(wo[:, :, :], I["Wo"].rearrange("(h p) d -> p h d", p=P)).then_inc(loaded, 16)
            sp.dma_start(o_norm[:, :], I["o_norm_w"].rearrange("(p a) -> p a", a=1)).then_inc(loaded, 16)
            sp.dma_start(mask_w[:, :, :], I["mask_w"]).then_inc(loaded, 16)
            sp.dma_start(mask_t[:, :, :], I["mask_t"]).then_inc(loaded, 16)
            with sp.Fori(0, NT) as t:
                sp.wait_ge(made["scanned"], NG * t)
                sp.dma_start(alpha[:, :], alpha_dram[bass.ds(t * H, H), :].rearrange("h n -> (h n)").partition_broadcast(P)).then_inc(alpha_in, 16)

        @block.tensor
        def _(pe):
            def fill(name, use, b, c, product, cols=P, at=0):
                wait_free(pe, name, use, b, c)
                for h in range(HG):
                    last = product(bank[name][:, at + h * cols:at + (h + 1) * cols], h)
                last.then_inc(filled[name], 1)

            def mm(lhsT, rhs_):
                return lambda out, h: nc.tensor.matmul(out, lhsT[:, h, :], rhs_[:, h, :], start=True, stop=True)

            def mm_half(lhsT, rhs_, l, which):
                return lambda out, h: nc.tensor.matmul(
                    out, lhsT[:, h, :], half(rhs_[:, :, :], l, which)[:, h, :, :], start=True, stop=True)

            def turn(x):
                return lambda out, h: nc.tensor.transpose(out, x[:, h, :], M.ident[:, :])

            def project(name, n, g, b, c):
                wait_free(pe, name, f"{name}{g}", b, c)
                wait_made(pe, "ht_copied", b, c, NG - 1)
                nc.tensor.matmul(bank[name][:, :], ht[:, :], w_all[:, n, g * 512:(g + 1) * 512],
                                 start=True, stop=True).then_inc(filled[name], 1)

            def turn_kq(g, b, c):
                wait_made(pe, "k_unit", b, c, g)
                fill("q", f"k_t{g}", b, c, turn(k_s[c % 2][g]))
                wait_made(pe, "q_unit", b, c, g)
                fill("k", f"q_t{g}", b, c, turn(q_s[g]))

            def keys_keys(g, b, c):
                wait_drained(pe, "q", f"k_t{g}", b, c)
                fill("v", f"KK{g}", b, c, mm(k_t[g], k_t[g]))

            def keys_queries(g, b, c):
                wait_drained(pe, "k", f"q_t{g}", b, c)
                fill("z", f"KQ{g}", b, c, mm(k_t[g], q_t[g]))

            def turn_l(g, b, c):
                wait_drained(pe, "v", f"KK{g}", b, c)
                fill(f"Z{g}", "L0", b, c, turn(neg_lt[g]))

            def front(b, c):
                for name, n in (("q", 0), ("k", 1), ("z", 3), ("v", 2)):
                    for g in range(NG):
                        project(name, n, g, b, c)
                for step in (turn_kq, keys_keys, keys_queries, turn_l):
                    for g in range(NG):
                        step(g, b, c)

            def back(b, c, ahead):
                for l in LV:
                    for g in range(NG):
                        wait_grown(pe, b, c, l - 1, g)
                        fill(f"Y{g}", f"Y{l}", b, c, mm_half(neg_lt[g], inv[g], l, LOW), P // 2)
                    if l == 1 and c:
                        for g in range(NG):
                            wait_drained(pe, f"Z{g}", "dS", b, c - 1)
                            fill(f"Z{g}", "KS", b, c, mm(k_t[g], state[g]))
                        for g in range(NG):
                            fill(f"Z{g}", "QS", b, c, mm(q_t[g], state[g]))
                    if ahead:
                        for g in range(NG):
                            if l == 1:
                                project("q", 0, g, *ahead)
                            if l == 2:
                                project("k", 1, g, *ahead)
                            if l == 3 + g:
                                project("z", 3, g, *ahead)
                            if l == 6:
                                turn_kq(g, *ahead)
                    for g in range(NG):
                        wait_drained(pe, f"Y{g}", f"Y{l}", b, c)
                        wait_free(pe, f"Z{g}", f"Z{l}", b, c)
                        if l == 1:
                            wait_made(pe, "w_t0", b, c, g)
                        if l < LEVELS - 1:
                            for h in range(HG):
                                mm_half(inv_t[g], y_s[g], l, LOW)(bank[f"Z{g}"][:, h * 64:(h + 1) * 64], h)
                        for h in range(HG):
                            last = mm_half(y_s[g], inv_t[g], l, HIGH)(bank[f"Z{g}"][:, 256 + h * 64:256 + (h + 1) * 64], h)
                        last.then_inc(filled[f"Z{g}"], 1)
                for g in range(NG):
                    wait_drained(pe, f"Z{g}", f"Z{LEVELS - 1}", b, c)
                    if c:
                        wait_made(pe, "rhs_ready", b, c, g)
                    else:
                        wait_drained(pe, "v", f"v{g}", b, c)
                    fill(f"Y{g}", "E", b, c, mm(inv_t[g], rhs[g] if c else v_s[g]))
                if ahead:
                    for g in range(NG):
                        project("v", 2, g, *ahead)
                    for g in range(NG):
                        keys_keys(g, *ahead)
                for g in range(NG):
                    wait_drained(pe, f"Y{g}", "E", b, c)
                    wait_drained(pe, "z", f"KQ{g}", b, c)
                    fill(f"Y{g}", "PD", b, c, mm(attn_t[g], delta[g]))
                for g in range(NG):
                    wait_made(pe, "delta_decayed", b, c, g)
                    fill(f"Z{g}", "dS", b, c, mm(k_s[c % 2][g], delta_d[g]))
                if ahead:
                    for g in range(NG):
                        keys_queries(g, *ahead)
                    for g in range(NG):
                        turn_l(g, *ahead)
                for g in range(NG):
                    wait_made(pe, "o_normed", b, c, g)
                    fill(f"Y{g}", "o_t", b, c, turn(o[g]))
                wait_free(pe, "Y0", "out", b, c)
                for g in range(NG):
                    wait_drained(pe, f"Y{g}", "o_t", b, c)
                    for h in range(HG):
                        last = nc.tensor.matmul(bank["Y0"][:, 0:D], o_t[g][:, h, :], wo[:, g * HG + h, :],
                                                start=(g + h == 0), stop=(g == NG - 1 and h == HG - 1))
                last.then_inc(filled["Y0"], 1)

            pe.wait_ge(loaded, 16 * 8)
            pe.wait_ge(prepared, 3)
            schedule(pe, front, back)

        @block.scalar
        def _(act):
            def copy_out(name, use, b, c, dest, func=ACT.Copy):
                wait_full(act, name, use, b, c)
                nc.scalar.activation(flat(dest), bank[name][:, :], func).then_inc(drained[name], 1)

            def silu(name, g, b, c):
                if name == "k":
                    copy_out("k", f"k{g}", b, c, k_s[c % 2][g], ACT.Silu)
                elif name == "z":
                    copy_out("z", f"z{g}", b, c, z_s[c % 2][g], ACT.Silu)
                else:
                    copy_out(name, f"{name}{g}", b, c, {"q": q_s, "v": v_s}[name][g], ACT.Silu)

            def roots(b, c):
                for g in range(NG):
                    wait_made(act, "sums", b, c, g)
                    nc.scalar.activation(root[:, g, 0, :], sum_sq[:, g, 0, :], ACT.Sqrt, bias=eps_q[:, :], scale=float(DK))
                    nc.scalar.activation(root[:, g, 1, :], sum_sq[:, g, 1, :], ACT.Sqrt, bias=eps_1[:, :]).then_inc(made["roots"], 1)

            def kq_turned(g, b, c):
                copy_out("q", f"k_t{g}", b, c, k_t[g])
                copy_out("k", f"q_t{g}", b, c, q_t[g])

            def unit_inverse(b, c):
                for g in range(NG):
                    if before(b, c):
                        wait_full(act, f"Y{g}", "E", *before(b, c))
                    nc.scalar.activation(flat(inv[g]), flat(four_ident), ACT.Copy)
                    nc.scalar.activation(flat(inv_t[g]), flat(four_ident), ACT.Copy).then_inc(made["inv_init"], 1)

            def front(b, c):
                for name in "qkzv":
                    for g in range(NG):
                        silu(name, g, b, c)
                roots(b, c)
                unit_inverse(b, c)
                for g in range(NG):
                    kq_turned(g, b, c)

            def back(b, c, ahead):
                for l in LV:
                    for g in range(NG):
                        wait_full(act, f"Y{g}", f"Y{l}", b, c)
                        nc.scalar.activation(half(y_s[g][:, :, :], l, LOW), packed(bank[f"Y{g}"][:, 0:256], l),
                                             ACT.Copy).then_inc(drained[f"Y{g}"], 1)
                    if ahead:
                        for g in range(NG):
                            if l == 1:
                                silu("q", g, *ahead)
                            if l == 2:
                                silu("k", g, *ahead)
                            if l == 3 + g:
                                silu("z", g, *ahead)
                        if l == 5:
                            roots(*ahead)
                        if l == 6:
                            for g in range(NG):
                                kq_turned(g, *ahead)
                if ahead:
                    for g in range(NG):
                        silu("v", g, *ahead)
                    unit_inverse(*ahead)
                for g in range(NG):
                    wait_made(act, "o_sums", b, c, g)
                    nc.scalar.activation(o_root[:, g, :], o_sum[:, g, :], ACT.Sqrt, bias=eps_1[:, :], scale=1.0 / DK).then_inc(made["o_roots"], 1)
                for g in range(NG):
                    copy_out(f"Y{g}", "o_t", b, c, o_t[g])

            act.wait_ge(prepared, 3)
            schedule(act, front, back)

        @block.gpsimd
        def _(pool):
            tt = nc.gpsimd.tensor_tensor

            def stage(b, c):
                if before(b, c):
                    wait_full(pool, "v", "v1", *before(b, c))
                pool.sem_inc(copy_wait_taken, 1)
                nc.gpsimd.tensor_copy(ht[:, :], M.HT[:, bass.ds(b, 1), c * P + 1:c * P + 1 + P].rearrange("p a n -> p (a n)")).then_inc(made["ht_copied"], NG)

            def decays(b, c):
                for g in range(NG):
                    wait_made(pool, "scanned", b, c, g)
                    pool.sem_inc(copy_wait_taken, 1)
                    nc.gpsimd.tensor_copy(end_decay[c % 2][:, g, :].unsqueeze(2), decay[g][:, :, P - 1:P])
                    tt(decay_b[g][:, :, :], decay[g][:, :, :], bc(per_token(T.minus_beta, b, c, g), P), ALU.mult).then_inc(made["decay_beta"], 1)

            def square(g, b, c):
                wait_drained(pool, "q", f"q{g}", b, c)
                tt(sq_q[g][:, :, :], q_s[g][:, :, :], q_s[g][:, :, :], ALU.mult)
                wait_drained(pool, "k", f"k{g}", b, c)
                tt(sq_k[g][:, :, :], k_s[c % 2][g][:, :, :], k_s[c % 2][g][:, :, :], ALU.mult).then_inc(made["squares"], 1)

            def unit_q(g, b, c):
                wait_made(pool, "units", b, c, g)
                tt(q_s[g][:, :, :], q_s[g][:, :, :], bc(unit[:, g, 0, :], P), ALU.mult).then_inc(made["q_unit"], 1)

            def front(b, c):
                stage(b, c)
                decays(b, c)
                for g in range(NG):
                    square(g, b, c)
                for g in range(NG):
                    unit_q(g, b, c)

            def back(b, c, ahead):
                if ahead:
                    stage(*ahead)
                    for g in range(NG):
                        square(g, *ahead)
                    for g in range(NG):
                        unit_q(g, *ahead)
                if c:
                    for g in range(NG):
                        wait_drained(pool, f"Z{g}", "dS", b, c - 1)
                        tt(state_g[g][:, :, :], state[g][:, :, :], bc(per_token(T.end, b, c, g), P), ALU.mult).then_inc(made["state_decayed"], 1)
                if ahead:
                    decays(*ahead)
                for g in range(NG):
                    wait_drained(pool, f"Y{g}", "E", b, c)
                    tt(delta_d[g][:, :, :], delta[g][:, :, :], bc(end_decay[c % 2][:, g, :], P), ALU.mult).then_inc(made["delta_decayed"], 1)
                for g in range(NG):
                    wait_drained(pool, f"Y{g}", "PD", b, c)
                    tt(rhs[g][:, :, :], o[g][:, :, :], o[g][:, :, :], ALU.mult).then_inc(made["o_squares"], 1)
                for g in range(NG):
                    wait_drained(pool, "z", f"z{g}", b, c)
                    tt(z_s[c % 2][g][:, :, :], z_s[c % 2][g][:, :, :], o[g][:, :, :], ALU.mult).then_inc(made["o_gated"], 1)

            for h in range(HG):
                last = nc.gpsimd.tensor_copy(four_ident[:, h, :], M.ident[:, :])
            last.then_inc(prepared, 1)
            for g in range(NG):
                last = nc.gpsimd.memset(flat(y_s[g]), 0.0)
            last.then_inc(prepared, 1)
            pool.wait_ge(prepared, 3)
            schedule(pool, front, back)

        @block.vector
        def _(dve):
            tt = nc.vector.tensor_tensor
            view = lambda x: x[:, :].rearrange("p (h n) -> p h n", n=P)

            def put(dest, which, mask, l, data):
                dve.sem_inc(wait_taken, 1)
                m = half(mask[:, l:l + 1, :], l, which).to_broadcast([P, HG, 64 >> l, 1 << l])
                return nc.vector.copy_predicated(half(dest[:, :, :], l, which), m, data)

            def scan(b, c):
                dve.wait_ge(alpha_in, 16 * (b * TPB + c) + 16)
                for g in range(NG):
                    nc.vector.tensor_tensor_scan(flat(decay[g]), alpha[:, g * 512:(g + 1) * 512], flat(four_ident),
                                                 0.0, ALU.mult, ALU.add).then_inc(made["scanned"], 1)

            def sums(g, b, c):
                wait_made(dve, "squares", b, c, g)
                nc.vector.tensor_reduce(sum_sq[:, g, 0, :], sq_q[g][:, :, :], AX.X, ALU.add)
                nc.vector.tensor_reduce(sum_sq[:, g, 1, :], sq_k[g][:, :, :], AX.X, ALU.add).then_inc(made["sums"], 1)

            def unit_k(g, b, c):
                wait_made(dve, "roots", b, c, g)
                nc.vector.reciprocal(unit[:, g, :, :], root[:, g, :, :]).then_inc(made["units"], 1)
                wait_made(dve, "units", b, c, g)
                k = k_s[c % 2][g]
                tt(k[:, :, :], k[:, :, :], bc(unit[:, g, 1, :], P), ALU.mult).then_inc(made["k_unit"], 1)

            def mask_keys(g, b, c):
                wait_full(dve, "v", f"KK{g}", b, c)
                wait_made(dve, "decay_beta", b, c, g)
                tt(neg_lt[g][:, :, :], view(bank["v"]), decay_b[g][:, :, :], ALU.mult).then_inc(drained["v"], 1)

            def mask_queries(g, b, c):
                wait_full(dve, "z", f"KQ{g}", b, c)
                wait_made(dve, "scanned", b, c, g)
                tt(attn_t[g][:, :, :], view(bank["z"]), decay[g][:, :, :], ALU.mult).then_inc(drained["z"], 1)

            def level_0(g, b, c):
                wait_made(dve, "inv_init", b, c, g)
                wait_drained(dve, "v", f"KK{g}", b, c)
                put(inv_t[g], HIGH, mask_t, 0, half(neg_lt[g][:, :, :], 0, HIGH)).then_inc(made["w_t0"], 1)
                wait_full(dve, f"Z{g}", "L0", b, c)
                put(inv[g], LOW, mask_w, 0, half(view(bank[f"Z{g}"]), 0, LOW)).then_inc(made["w_grown"], 1)
                wait_grown(dve, b, c, 0, g)
                dve.sem_inc(drained[f"Z{g}"], 1)

            def front(b, c):
                scan(b, c)
                for step in (sums, unit_k, mask_keys, mask_queries, level_0):
                    for g in range(NG):
                        step(g, b, c)

            def back(b, c, ahead):
                for l in LV:
                    if l == 1 and c:
                        for g in range(NG):
                            wait_full(dve, f"Z{g}", "KS", b, c)
                            tt(rhs[g][:, :, :], view(bank[f"Z{g}"]), bc(per_token(T.g, b, c, g), P), ALU.mult).then_inc(drained[f"Z{g}"], 1)
                        for g in range(NG):
                            wait_full(dve, f"Z{g}", "QS", b, c)
                            tt(o[g][:, :, :], view(bank[f"Z{g}"]), bc(per_token(T.g, b, c, g), P), ALU.mult).then_inc(drained[f"Z{g}"], 1)
                    for g in range(NG):
                        wait_full(dve, f"Z{g}", f"Z{l}", b, c)
                        if l < LEVELS - 1:
                            put(inv[g], LOW, mask_w, l, packed(bank[f"Z{g}"][:, 0:256], l)).then_inc(made["w_grown"], 1)
                        put(inv_t[g], HIGH, mask_t, l, packed(bank[f"Z{g}"][:, 256:512], l)).then_inc(drained[f"Z{g}"], 1)
                    if l == 1 and c:
                        for g in range(NG):
                            wait_drained(dve, f"Z{g}", "KS", b, c)
                            wait_drained(dve, "v", f"v{g}", b, c)
                            tt(rhs[g][:, :, :], v_s[g][:, :, :], rhs[g][:, :, :], ALU.subtract).then_inc(made["rhs_ready"], 1)
                    if ahead:
                        if l == 2:
                            scan(*ahead)
                        if l == 4:
                            for g in range(NG):
                                sums(g, *ahead)
                        if l == 5:
                            for g in range(NG):
                                unit_k(g, *ahead)
                for g in range(NG):
                    wait_full(dve, f"Y{g}", "E", b, c)
                    tt(delta[g][:, :, :], view(bank[f"Y{g}"]), bc(per_token(T.beta, b, c, g), P), ALU.mult).then_inc(drained[f"Y{g}"], 1)
                if ahead:
                    for g in range(NG):
                        mask_keys(g, *ahead)
                for g in range(NG):
                    wait_full(dve, f"Y{g}", "PD", b, c)
                    if c:
                        wait_drained(dve, f"Z{g}", "QS", b, c)
                        tt(o[g][:, :, :], view(bank[f"Y{g}"]), o[g][:, :, :], ALU.add).then_inc(drained[f"Y{g}"], 1)
                    else:
                        nc.vector.tensor_copy(flat(o[g]), bank[f"Y{g}"][:, :]).then_inc(drained[f"Y{g}"], 1)
                for g in range(NG):
                    wait_full(dve, f"Z{g}", "dS", b, c)
                    if c:
                        wait_made(dve, "state_decayed", b, c, g)
                        tt(state[g][:, :, :], view(bank[f"Z{g}"]), state_g[g][:, :, :], ALU.add).then_inc(drained[f"Z{g}"], 1)
                    else:
                        nc.vector.tensor_copy(flat(state[g]), bank[f"Z{g}"][:, :]).then_inc(drained[f"Z{g}"], 1)
                for g in range(NG):
                    wait_made(dve, "o_squares", b, c, g)
                    nc.vector.tensor_reduce(o_sum[:, g, :], rhs[g][:, :, :], AX.X, ALU.add).then_inc(made["o_sums"], 1)
                if ahead:
                    for g in range(NG):
                        mask_queries(g, *ahead)
                    for g in range(NG):
                        level_0(g, *ahead)
                for g in range(NG):
                    wait_made(dve, "o_roots", b, c, g)
                    nc.vector.reciprocal(o_unit[:, g, :], o_root[:, g, :]).then_inc(made["o_units"], 1)
                    wait_made(dve, "o_units", b, c, g)
                    wait_made(dve, "o_gated", b, c, g)
                    tt(o[g][:, :, :], z_s[c % 2][g][:, :, :], bc(o_unit[:, g, :], P), ALU.mult).then_inc(made["o_normed"], 1)
                wait_full(dve, "Y0", "out", b, c)
                x1 = M.X1[:, bass.ds(b * TPB + c, 1), :].rearrange("p a d -> p (a d)")
                tt(x1, bank["Y0"][:, 0:D], x1, ALU.add).then_inc(drained["Y0"], 1)

            dve.wait_ge(loaded, 16 * 8)
            nc.vector.memset(eps_q[:, :], float(DK) * 1e-6)
            nc.vector.memset(eps_1[:, :], 1e-6)
            nc.vector.tensor_scalar(flat(wo), flat(wo), o_norm[:, :], None, ALU.mult).then_inc(prepared, 1)
            dve.wait_ge(prepared, 3)
            schedule(dve, front, back)


def ffn_phase(nc, M, I, tag, w_in, w_out):
    with Space(nc, tag) as s:
        win = s.sb("win", [P, FF])
        wout = s.sb("wout", [P, NF, D])
        act_buf = s.sb("relu", [P, NF, S])
        hid = s.sb("hid", [P, NF, S])
        res = s.sb("res", [P, TPB, D])
        up = [s.ps(f"up{f}") for f in range(NF)]
        down = s.ps("down")
        w_loaded = s.sem("w_loaded")
        up_ready, relu_ready, hid_ready, down_ready, res_ready, x_ready = (
            s.sem(n) for n in ("up_ready", "relu_ready", "hid_ready", "down_ready", "res_ready", "x_ready"))
        block = s.block()

        @block.sync
        def _(sp):
            sp.dma_start(win[:, :], w_in).then_inc(w_loaded, 16)
            sp.dma_start(wout[:, :, :], w_out.rearrange("(f p) d -> p f d", p=P)).then_inc(w_loaded, 16)

        @block.tensor
        def _(pe):
            pe.wait_ge(w_loaded, 32)
            with pe.Fori(0, B) as b:
                for f in range(NF):
                    pe.wait_ge(relu_ready, NF * b + f + 1)
                    nc.tensor.matmul(up[f][:, :], win[:, f * P:(f + 1) * P], M.HT[:, bass.ds(b, 1), 1:1 + S].rearrange("p a n -> p (a n)"),
                                     start=True, stop=True).then_inc(up_ready, 1)
                pe.wait_ge(hid_ready, NF * (b + 1))
                pe.wait_ge(res_ready, b + 1)
                for j in range(TPB):
                    for f in range(NF):
                        last = nc.tensor.matmul(down[:, j * P:(j + 1) * P], hid[:, f, j * P:(j + 1) * P], wout[:, f, :],
                                                start=(f == 0), stop=(f == NF - 1))
                last.then_inc(down_ready, 1)

        @block.scalar
        def _(act):
            act.sem_inc(relu_ready, NF)
            with act.Fori(0, B) as b:
                for f in range(NF):
                    act.wait_ge(up_ready, NF * b + f + 1)
                    act.wait_ge(hid_ready, NF * b)
                    nc.scalar.activation(act_buf[:, f, :], up[f][:, :], ACT.Relu).then_inc(relu_ready, 1)

        @block.vector
        def _(dve):
            dve.sem_inc(res_ready, 1)
            with dve.Fori(0, B) as b:
                for f in range(NF):
                    dve.wait_ge(relu_ready, NF * b + f + 1 + NF)
                    nc.vector.tensor_tensor(hid[:, f, :], act_buf[:, f, :], act_buf[:, f, :], ALU.mult).then_inc(hid_ready, 1)
                dve.wait_ge(down_ready, b + 1)
                ts = bass.ds(b * TPB, TPB)
                nc.vector.tensor_tensor(res[:, :, :].rearrange("p t d -> p (t d)"), down[:, :],
                                        M.X1[:, ts, :].rearrange("p t d -> p (t d)"), ALU.add).then_inc(res_ready, 1)
                dve.wait_ge(res_ready, b + 2)
                nc.vector.tensor_tensor(M.X[:, ts, :], M.X[:, ts, :], res[:, :, :], ALU.add).then_inc(x_ready, 1)

def moe_phase(nc, M, I, tag):
    with Space(nc, tag) as g:
        gate_tok = g.sb("gate_tok", [P, TPB, E, B])
        gate_dram = nc.dram_tensor(tag + "_gate_dram", [P, S], F32, kind="Internal").ap()
        w1 = g.sb("w1", [P, E, FF])
        w2 = g.sb("w2", [P, E, NF, D])
        b1 = g.sb("b1", [P, E, NF])
        b2 = g.sb("b2", [E, D])

        with Space(nc, tag + "r") as s:
            wg = s.sb("wg", [P, E])
            logits = [s.sb(f"logits{p}", [E, S]) for p in range(2)]
            score = s.sb("score", [P, S])
            expo = s.sb("expo", [P, S])
            above = s.sb("above", [P, S])
            equal = s.sb("equal", [P, S])
            rank = s.sb("rank", [P, S])
            gate = s.sb("gate", [P, S])
            group_ones = s.sb("group_ones", [P, P])
            before_ones = s.sb("before_ones", [P, P])
            bit_int = s.sb("bit_int", [P, BITS], I32)
            bit_val = s.sb("bit_val", [P, BITS])
            best = s.sb("best", [P, 1], I32)
            trial = s.sb("trial", [P, 1], I32)
            step = s.sb("step", [P, 1], I32)
            count = s.sb("count", [P, 1])
            sums = s.sb("sums", [P, 2])
            room = s.sb("room", [P, 1])
            logit_dram = nc.dram_tensor(tag + "_logit_dram", [E, NT * P], F32, kind="Internal").ap()
            lg = [s.ps(f"lg{p}", [E, 512]) for p in range(2)]
            tot = s.ps("tot")
            gt = s.ps("gt")
            (loaded, w_loaded, lg_ready, lg_copied, score_in, expo_ready, chain, counted, totalled,
             gate_ready, gate_out, turned, tie_ready, before_ready) = (s.sem(n) for n in (
                 "loaded", "w_loaded", "lg_ready", "lg_copied", "score_in", "expo_ready", "chain",
                 "counted", "totalled", "gate_ready", "gate_out", "turned", "tie_ready", "before_ready"))
            logit_out = [s.sem(f"logit_out{p}") for p in range(2)]
            block = s.block()

            @block.sync
            def _(sp):
                sp.dma_start(wg[:, :], I["Wg_moe"]).then_inc(loaded, 16)
                sp.dma_start(group_ones[:, :], I["group_ones"]).then_inc(loaded, 16)
                sp.dma_start(before_ones[:, :], I["before_ones"]).then_inc(loaded, 16)
                sp.dma_start(bit_int[:, :], I["bit_int"]).then_inc(loaded, 16)
                sp.dma_start(bit_val[:, :], I["bit_val"]).then_inc(loaded, 16)
                with sp.Fori(0, B // 2) as i:
                    for p in range(2):
                        sp.wait_ge(lg_copied, 2 * i + p + 3)
                        sp.dma_start(logit_dram[:, bass.ds((2 * i + p) * S, S)], logits[p][:, :]).then_inc(logit_out[p], 16)
                for p in range(2):
                    sp.wait_ge(logit_out[p], 16 * (B // 2))
                sp.dma_start(score[:, :], logit_dram.rearrange("e (b n) -> (e b) n", n=S)).then_inc(score_in, 16)
                sp.wait_ge(gate_ready, 1)
                sp.dma_start(gate_dram, gate[:, :]).then_inc(gate_out, 16)
                sp.wait_ge(gate_out, 16)

            @block.gpsimd
            def _(pool):
                pool.dma_start(w1[:, :, :], I["W1"].rearrange("e d f -> d e f")).then_inc(w_loaded, 16)
                pool.dma_start(w2[:, :, :, :], I["W2"].rearrange("e (f p) d -> p e f d", p=P)).then_inc(w_loaded, 16)
                pool.dma_start(b1[:, :, :], I["b1"]).then_inc(w_loaded, 16)
                pool.dma_start(b2[:, :], I["b2"]).then_inc(w_loaded, 16)
                pool.wait_ge(w_loaded, 64)

            @block.scalar
            def _(act):
                act.wait_ge(score_in, 16)
                nc.scalar.activation(rank[:, :], score[:, :], ACT.Abs).then_inc(expo_ready, 1)
                act.wait_ge(expo_ready, 1)
                nc.scalar.activation(expo[:, :], rank[:, :], ACT.Exp, scale=-1.0).then_inc(expo_ready, 1)

            @block.tensor
            def _(pe):
                pe.wait_ge(loaded, 80)
                with pe.Fori(0, B // 2) as i:
                    for p in range(2):
                        pe.wait_ge(lg_copied, 2 * i + p + 1)
                        nc.tensor.matmul(lg[p][:, :], wg[:, :], M.HT[:, bass.ds(2 * i + p, 1), 1:1 + S].rearrange("p a n -> p (a n)"),
                                         start=True, stop=True).then_inc(lg_ready, 1)
                with pe.Fori(0, BITS + 1) as i:
                    pe.wait_ge(counted, i + 1)
                    nc.tensor.matmul(tot[:, 0:1], group_ones[:, :], count[:, :], start=True, stop=True).then_inc(totalled, 1)
                pe.wait_ge(tie_ready, 1)
                nc.tensor.matmul(tot[:, 1:2], before_ones[:, :], count[:, :], start=True, stop=True).then_inc(before_ready, 1)
                pe.wait_ge(gate_ready, 1)
                for c in range(TPB):
                    last = nc.tensor.transpose(gt[:, c * P:(c + 1) * P], gate[:, c * P:(c + 1) * P], M.ident[:, :])
                last.then_inc(turned, 1)

            @block.vector
            def _(dve):
                links = [0]

                def link(ins):
                    ins.then_inc(chain, 1)
                    links[0] += 1
                    dve.wait_ge(chain, links[0])

                dve.sem_inc(lg_copied, 2)
                with dve.Fori(0, B // 2) as i:
                    for p in range(2):
                        dve.wait_ge(lg_ready, 2 * i + p + 1)
                        dve.wait_ge(logit_out[p], 16 * i)
                        nc.vector.tensor_copy(logits[p][:, :], lg[p][:, :]).then_inc(lg_copied, 1)
                link(nc.vector.memset(best[:, :], 0))
                dve.wait_ge(expo_ready, 2)
                link(nc.vector.tensor_scalar(above[:, :], score[:, :], 0.0, None, ALU.is_ge))
                link(nc.vector.tensor_scalar(equal[:, :], expo[:, :], 1.0, None, ALU.add))
                link(nc.vector.reciprocal(rank[:, :], equal[:, :]))
                link(nc.vector.tensor_tensor(score[:, :], rank[:, :], expo[:, :], ALU.mult))
                link(nc.vector.copy_predicated(score[:, :], above[:, :].bitcast(I32), rank[:, :]))
                with dve.Fori(0, BITS) as i:
                    nc.vector.tensor_tensor(trial[:, :], best[:, :], bit_int[:, bass.ds(i, 1)], ALU.bitwise_or).then_inc(chain, 1)
                    dve.wait_ge(chain, 3 * i + (links[0] + 1))
                    nc.vector.tensor_scalar(above[:, :], score[:, :], trial[:, :].bitcast(F32), 0.0, ALU.is_ge, ALU.add,
                                            accum_out=count[:, :]).then_inc(counted, 1)
                    dve.wait_ge(totalled, i + 1)
                    nc.vector.tensor_scalar(step[:, :], tot[:, 0:1], float(CAP), bit_val[:, bass.ds(i, 1)],
                                            ALU.is_ge, ALU.mult).then_inc(chain, 1)
                    dve.wait_ge(chain, 3 * i + (links[0] + 2))
                    nc.vector.tensor_tensor(best[:, :], best[:, :], step[:, :], ALU.bitwise_or).then_inc(chain, 1)
                    dve.wait_ge(chain, 3 * i + (links[0] + 3))
                links[0] += 3 * BITS
                nc.vector.tensor_scalar(above[:, :], score[:, :], best[:, :].bitcast(F32), 0.0, ALU.is_gt, ALU.add,
                                        accum_out=count[:, :]).then_inc(counted, 1)
                dve.wait_ge(totalled, BITS + 1)
                nc.vector.tensor_scalar(equal[:, :], score[:, :], best[:, :].bitcast(F32), 0.0, ALU.is_equal, ALU.add,
                                        accum_out=count[:, :]).then_inc(tie_ready, 1)
                dve.wait_ge(tie_ready, 1)
                link(nc.vector.tensor_tensor_scan(rank[:, :], equal[:, :], equal[:, :], 0.0, ALU.add, ALU.bypass))
                dve.wait_ge(before_ready, 1)
                link(nc.vector.tensor_copy(sums[:, :], tot[:, 0:2]))
                link(nc.vector.tensor_tensor(room[:, :], sums[:, 0:1], sums[:, 1:2], ALU.add))
                link(nc.vector.tensor_scalar(room[:, :], room[:, :], -1.0, float(CAP), ALU.mult, ALU.add))
                link(nc.vector.tensor_scalar(rank[:, :], rank[:, :], room[:, :], None, ALU.is_le))
                link(nc.vector.tensor_tensor(rank[:, :], rank[:, :], equal[:, :], ALU.mult))
                link(nc.vector.tensor_tensor(rank[:, :], rank[:, :], above[:, :], ALU.add))
                nc.vector.tensor_tensor(gate[:, :], rank[:, :], score[:, :], ALU.mult).then_inc(gate_ready, 1)
                dve.wait_ge(turned, 1)
                nc.vector.tensor_copy(gate_tok[:, :, :, :].rearrange("p c e b -> p (c e b)"), gt[:, :])

        with Space(nc, tag + "x") as s:
            hid = [s.sb(f"hid{p}", [P, NF, S]) for p in range(2)]
            gate_now = s.sb("gate_now", [E, S])
            gate_view = gate_dram.rearrange("(e b) n -> e b n", e=E)
            up = [s.ps(f"up{p}") for p in range(4)]
            down = [s.ps(f"down{p}") for p in range(2)]
            bias = s.ps("bias")
            (up_ready, hid_ready, down_ready, added, now_ready, bias_ready) = (s.sem(n) for n in (
                "up_ready", "hid_ready", "down_ready", "added", "now_ready", "bias_ready"))
            block = s.block()
            PER = E + 1

            @block.sync
            def _(sp):
                with sp.Fori(0, B) as b:
                    sp.wait_ge(bias_ready, b)
                    sp.dma_start(gate_now[:, :], gate_view[:, bass.ds(b, 1), :].rearrange("e b n -> e (b n)")).then_inc(now_ready, 16)

            @block.tensor
            def _(pe):
                def lift(b, e):
                    for f in range(NF):
                        pe.wait_ge(hid_ready, E * NF * b + NF * e + f + 1)
                        nc.tensor.matmul(up[f][:, :], w1[:, e, f * P:(f + 1) * P], M.HT[:, bass.ds(b, 1), 1:1 + S].rearrange("p a n -> p (a n)"),
                                         start=True, stop=True).then_inc(up_ready, 1)

                with pe.Fori(0, B) as b:
                    lift(b, 0)
                    pe.wait_ge(now_ready, 16 * b + 16)
                    pe.wait_ge(added, PER * b)
                    for j in range(TPB):
                        last = nc.tensor.matmul(bias[:, j * P:(j + 1) * P], gate_now[:, j * P:(j + 1) * P], b2[:, :], start=True, stop=True)
                    last.then_inc(bias_ready, 1)
                    for e in range(E):
                        if e + 1 < E:
                            lift(b, e + 1)
                        pe.wait_ge(hid_ready, E * NF * b + NF * e + 2 * NF)
                        pe.wait_ge(added, PER * b + max(e, 1))
                        for j in range(TPB):
                            for f in range(NF):
                                last = nc.tensor.matmul(down[e % 2][:, j * P:(j + 1) * P], hid[e % 2][:, f, j * P:(j + 1) * P],
                                                        w2[:, e, f, :], start=(f == 0), stop=(f == NF - 1))
                        last.then_inc(down_ready, 1)

            @block.scalar
            def _(act):
                act.sem_inc(hid_ready, NF)
                with act.Fori(0, B) as b:
                    for e in range(E):
                        for f in range(NF):
                            act.wait_ge(up_ready, E * NF * b + NF * e + f + 1)
                            act.wait_ge(down_ready, E * b + max(e - 1, 0))
                            nc.scalar.activation(hid[e % 2][:, f, :], up[f][:, :], ACT.Gelu, bias=b1[:, e, f:f + 1]).then_inc(hid_ready, 1)

            @block.vector
            def _(dve):
                with dve.Fori(0, B) as b:
                    dve.wait_ge(bias_ready, b + 1)
                    dve.wait_ge(added, PER * b)
                    ts = bass.ds(b * TPB, TPB)
                    nc.vector.tensor_tensor(M.X[:, ts, :].rearrange("p t d -> p (t d)"), bias[:, :],
                                            M.X[:, ts, :].rearrange("p t d -> p (t d)"), ALU.add).then_inc(added, 1)
                    for e in range(E):
                        dve.wait_ge(down_ready, E * b + e + 1)
                        dve.wait_ge(added, PER * b + e + 1)
                        for j in range(TPB):
                            t1 = bass.ds(b * TPB + j, 1)
                            last = nc.vector.scalar_tensor_tensor(M.X[:, t1, :].rearrange("p t d -> p (t d)"), down[e % 2][:, j * P:(j + 1) * P],
                                                                  gate_tok[:, j, e, bass.ds(b, 1)], M.X[:, t1, :].rearrange("p t d -> p (t d)"),
                                                                  ALU.mult, ALU.add)
                        last.then_inc(added, 1)

def rwkv_mix_phase(nc, M, I, V):
    with Space(nc, "tm") as s:
        w_raw = [s.sb(f"w_raw{n}", [P, D]) for n in range(3)]
        w_mix = [s.sb(f"w_mix{n}", [P, D]) for n in range(3)]
        w_old = [s.sb(f"w_old{n}", [P, D]) for n in range(3)]
        wo = s.sb("wo", [P, D])
        one_less = s.sb("one_less", [P, 3])
        decay = s.sb("decay", [P, 1])
        decay_row = s.sb("decay_row", [P, S])
        ks = [s.sb(f"k{p}", [P, S]) for p in range(2)]
        vs = [s.sb(f"v{p}", [P, S]) for p in range(2)]
        rs = [s.sb(f"r{p}", [P, S]) for p in range(2)]
        peak = s.sb("peak", [P, 1 + S])
        num = s.sb("num", [P, 1 + S])
        den = s.sb("den", [P, 1 + S])
        a_keep, a_new, p_keep, p_new, top = (s.sb(n, [P, S]) for n in ("a_keep", "a_new", "p_keep", "p_new", "top"))
        e_keep, e_new, f_keep, f_new = (s.sb(n, [P, S]) for n in ("e_keep", "e_new", "f_keep", "f_new"))
        ev, fv, fa, fb = (s.sb(n, [P, S]) for n in ("ev", "fv", "fa", "fb"))
        y = s.sb("y", [P, S])
        kvr = [s.ps(f"kvr{n}") for n in range(3)]
        att = s.ps("att")
        (loaded, chain, w_ready, decay_exp, kvr_ready, k_ready, v_ready, r_ready, args_ready, args2_ready, exps_ready,
         ev_ready, fv_ready, y_ready, att_ready, added, done) = (s.sem(n) for n in (
             "loaded", "chain", "w_ready", "decay_exp", "kvr_ready", "k_ready", "v_ready", "r_ready", "args_ready",
             "args2_ready", "exps_ready", "ev_ready", "fv_ready", "y_ready", "att_ready", "added", "done"))
        block = s.block()
        LINKS = 10

        @block.sync
        def _(sp):
            for n, name in enumerate(("wk", "wv", "wr")):
                sp.dma_start(w_raw[n][:, :], I[name]).then_inc(loaded, 16)
            sp.dma_start(wo[:, :], I["wo"]).then_inc(loaded, 16)

        @block.tensor
        def _(pe):
            pe.wait_ge(w_ready, 1)
            with pe.Fori(0, B) as b:
                for n, freed in enumerate((k_ready, v_ready, r_ready)):
                    pe.wait_ge(freed, b)
                    nc.tensor.matmul(kvr[n][:, :], w_mix[n][:, :], M.HT[:, bass.ds(b, 1), 1:1 + S].rearrange("p a n -> p (a n)"),
                                     start=True, stop=False)
                    nc.tensor.matmul(kvr[n][:, :], w_old[n][:, :], M.HT[:, bass.ds(b, 1), 0:S].rearrange("p a n -> p (a n)"),
                                     start=False, stop=True).then_inc(kvr_ready, 1)
                pe.wait_ge(y_ready, b + 1)
                pe.wait_ge(added, b)
                for j in range(TPB):
                    last = nc.tensor.matmul(att[:, j * P:(j + 1) * P], y[:, j * P:(j + 1) * P], wo[:, :], start=True, stop=True)
                last.then_inc(att_ready, 1)

        @block.scalar
        def _(act):
            nc.scalar.activation(decay[:, :], V("time_decay"), ACT.Exp).then_inc(decay_exp, 1)
            with act.Fori(0, B // 2) as i:
                for p in range(2):
                    b = 2 * i + p
                    act.wait_ge(y_ready, b)
                    act.wait_ge(kvr_ready, 3 * b + 1)
                    nc.scalar.activation(ks[p][:, :], kvr[0][:, :], ACT.Copy).then_inc(k_ready, 1)
                    act.wait_ge(kvr_ready, 3 * b + 2)
                    nc.scalar.activation(vs[p][:, :], kvr[1][:, :], ACT.Copy).then_inc(v_ready, 1)
                    act.wait_ge(kvr_ready, 3 * b + 3)
                    nc.scalar.activation(rs[p][:, :], kvr[2][:, :], ACT.Sigmoid).then_inc(r_ready, 1)
                    act.wait_ge(args_ready, b + 1)
                    nc.scalar.activation(e_keep[:, :], a_keep[:, :], ACT.Exp, bias=V("w")).then_inc(exps_ready, 1)
                    nc.scalar.activation(e_new[:, :], a_new[:, :], ACT.Exp).then_inc(exps_ready, 1)
                    act.wait_ge(args2_ready, b + 1)
                    nc.scalar.activation(f_keep[:, :], p_keep[:, :], ACT.Exp).then_inc(exps_ready, 1)
                    nc.scalar.activation(f_new[:, :], p_new[:, :], ACT.Exp, bias=V("time_first")).then_inc(exps_ready, 1)

        @block.gpsimd
        def _(pool):
            with pool.Fori(0, B // 2) as i:
                for p in range(2):
                    b = 2 * i + p
                    pool.wait_ge(exps_ready, 4 * b + 2)
                    pool.wait_ge(v_ready, b + 1)
                    nc.gpsimd.tensor_tensor(ev[:, :], e_new[:, :], vs[p][:, :], ALU.mult).then_inc(ev_ready, 1)
                    pool.wait_ge(exps_ready, 4 * b + 4)
                    nc.gpsimd.tensor_tensor(fv[:, :], f_new[:, :], vs[p][:, :], ALU.mult).then_inc(fv_ready, 1)

        @block.vector
        def _(dve):
            dve.wait_ge(loaded, 64)
            nc.vector.memset(peak[:, 0:1], -1e38)
            nc.vector.memset(num[:, 0:1], 0.0)
            nc.vector.memset(den[:, 0:1], 0.0)
            dve.wait_ge(decay_exp, 1)
            nc.vector.tensor_scalar(one_less[:, :], V("tm_mix"), -1.0, 1.0, ALU.mult, ALU.add).then_inc(chain, 1)
            nc.vector.tensor_scalar(V("w"), decay[:, :], -1.0, None, ALU.mult).then_inc(chain, 1)
            dve.wait_ge(chain, 2)
            nc.vector.memset(decay_row[:, :], 0.0).then_inc(chain, 1)
            dve.wait_ge(chain, 3)
            nc.vector.tensor_scalar(decay_row[:, :], decay_row[:, :], V("w"), None, ALU.add).then_inc(chain, 1)
            for n in range(3):
                nc.vector.tensor_scalar(w_mix[n][:, :], w_raw[n][:, :], V("tm_mix")[:, n:n + 1], None, ALU.mult)
                last = nc.vector.tensor_scalar(w_old[n][:, :], w_raw[n][:, :], one_less[:, n:n + 1], None, ALU.mult)
            last.then_inc(w_ready, 1)
            dve.wait_ge(chain, 4)
            with dve.Fori(0, B // 2) as i:
                for p in range(2):
                    b = 2 * i + p
                    at = [0]

                    def link(ins):
                        at[0] += 1
                        ins.then_inc(chain, 1)
                        dve.wait_ge(chain, LINKS * b + 4 + at[0])

                    k, r = ks[p], rs[p]
                    dve.wait_ge(k_ready, b + 1)
                    link(nc.vector.tensor_tensor_scan(peak[:, 1:], decay_row[:, :], k[:, :], -1e38, ALU.add, ALU.max))
                    nc.vector.tensor_tensor(a_keep[:, :], peak[:, 0:S], peak[:, 1:], ALU.subtract)
                    nc.vector.tensor_tensor(a_new[:, :], k[:, :], peak[:, 1:], ALU.subtract).then_inc(args_ready, 1)
                    link(nc.vector.scalar_tensor_tensor(top[:, :], k[:, :], V("time_first"), peak[:, 0:S], ALU.add, ALU.max))
                    nc.vector.tensor_tensor(p_keep[:, :], peak[:, 0:S], top[:, :], ALU.subtract)
                    nc.vector.tensor_tensor(p_new[:, :], k[:, :], top[:, :], ALU.subtract).then_inc(args2_ready, 1)
                    dve.wait_ge(exps_ready, 4 * b + 2)
                    link(nc.vector.tensor_tensor_scan(den[:, 1:], e_keep[:, :], e_new[:, :], 0.0, ALU.mult, ALU.add))
                    dve.wait_ge(ev_ready, b + 1)
                    link(nc.vector.tensor_tensor_scan(num[:, 1:], e_keep[:, :], ev[:, :], 0.0, ALU.mult, ALU.add))
                    dve.wait_ge(exps_ready, 4 * b + 4)
                    link(nc.vector.tensor_tensor(fb[:, :], f_keep[:, :], den[:, 0:S], ALU.mult))
                    link(nc.vector.tensor_tensor(fb[:, :], fb[:, :], f_new[:, :], ALU.add))
                    link(nc.vector.reciprocal(top[:, :], fb[:, :]))
                    link(nc.vector.tensor_tensor(fa[:, :], f_keep[:, :], num[:, 0:S], ALU.mult))
                    dve.wait_ge(fv_ready, b + 1)
                    link(nc.vector.tensor_tensor(fa[:, :], fa[:, :], fv[:, :], ALU.add))
                    link(nc.vector.tensor_tensor(fa[:, :], fa[:, :], top[:, :], ALU.mult))
                    dve.wait_ge(r_ready, b + 1)
                    nc.vector.tensor_tensor(y[:, :], fa[:, :], r[:, :], ALU.mult).then_inc(y_ready, 1)
                    assert at[0] == LINKS
                    dve.wait_ge(att_ready, b + 1)
                    ts = bass.ds(b * TPB, TPB)
                    nc.vector.tensor_tensor(M.X1[:, ts, :].rearrange("p t d -> p (t d)"), att[:, :],
                                            M.X1[:, ts, :].rearrange("p t d -> p (t d)"), ALU.add).then_inc(added, 1)


def rwkv_channel_phase(nc, M, I, V):
    with Space(nc, "cm") as s:
        cwk = s.sb("cwk", [P, FF])
        cwv = s.sb("cwv", [P, NF, D])
        cwr = s.sb("cwr", [P, D])
        change = s.sb("change", [P, S])
        mixed_k = s.sb("mixed_k", [P, S])
        mixed_r = s.sb("mixed_r", [P, S])
        relu = s.sb("relu", [P, NF, S])
        hid = s.sb("hid", [P, NF, S])
        rr = s.sb("rr", [P, S])
        res = s.sb("res", [P, S])
        up = [s.ps(f"up{f}") for f in range(NF)]
        down = s.ps("down")
        rps = s.ps("rps")
        (loaded, change_ready, mixed_ready, up_ready, relu_ready, hid_ready, r_ready, rr_ready, down_ready, chain,
         added) = (s.sem(n) for n in ("loaded", "change_ready", "mixed_ready", "up_ready", "relu_ready", "hid_ready",
                                      "r_ready", "rr_ready", "down_ready", "chain", "added"))
        block = s.block()

        @block.sync
        def _(sp):
            sp.dma_start(cwk[:, :], I["cwk"]).then_inc(loaded, 16)
            sp.dma_start(cwv[:, :, :], I["cwv"].rearrange("(f p) d -> p f d", p=P)).then_inc(loaded, 16)
            sp.dma_start(cwr[:, :], I["cwr"]).then_inc(loaded, 16)

        @block.tensor
        def _(pe):
            pe.wait_ge(loaded, 48)
            with pe.Fori(0, B) as b:
                pe.wait_ge(mixed_ready, 2 * b + 1)
                for f in range(NF):
                    pe.wait_ge(relu_ready, NF * b + f + 1)
                    nc.tensor.matmul(up[f][:, :], cwk[:, f * P:(f + 1) * P], mixed_k[:, :], start=True, stop=True).then_inc(up_ready, 1)
                pe.wait_ge(mixed_ready, 2 * b + 2)
                pe.wait_ge(rr_ready, b)
                for j in range(TPB):
                    last = nc.tensor.matmul(rps[:, j * P:(j + 1) * P], mixed_r[:, j * P:(j + 1) * P], cwr[:, :], start=True, stop=True)
                last.then_inc(r_ready, 1)
                pe.wait_ge(hid_ready, NF * (b + 1))
                pe.wait_ge(chain, 2 * b)
                for j in range(TPB):
                    for f in range(NF):
                        last = nc.tensor.matmul(down[:, j * P:(j + 1) * P], hid[:, f, j * P:(j + 1) * P], cwv[:, f, :],
                                                start=(f == 0), stop=(f == NF - 1))
                last.then_inc(down_ready, 1)

        @block.gpsimd
        def _(pool):
            with pool.Fori(0, B) as b:
                pool.wait_ge(mixed_ready, 2 * b)
                nc.gpsimd.tensor_tensor(change[:, :], M.HT[:, bass.ds(b, 1), 1:1 + S].rearrange("p a n -> p (a n)"),
                                        M.HT[:, bass.ds(b, 1), 0:S].rearrange("p a n -> p (a n)"), ALU.subtract).then_inc(change_ready, 1)

        @block.scalar
        def _(act):
            act.sem_inc(relu_ready, NF)
            with act.Fori(0, B) as b:
                for f in range(NF):
                    act.wait_ge(up_ready, NF * b + f + 1)
                    act.wait_ge(hid_ready, NF * b)
                    nc.scalar.activation(relu[:, f, :], up[f][:, :], ACT.Relu).then_inc(relu_ready, 1)
                act.wait_ge(r_ready, b + 1)
                act.wait_ge(added, b)
                nc.scalar.activation(rr[:, :], rps[:, :], ACT.Sigmoid).then_inc(rr_ready, 1)

        @block.vector
        def _(dve):
            with dve.Fori(0, B) as b:
                old = M.HT[:, bass.ds(b, 1), 0:S].rearrange("p a n -> p (a n)")
                dve.wait_ge(change_ready, b + 1)
                dve.wait_ge(r_ready, b)
                nc.vector.scalar_tensor_tensor(mixed_k[:, :], change[:, :], V("cm_mix_k"), old, ALU.mult, ALU.add).then_inc(mixed_ready, 1)
                nc.vector.scalar_tensor_tensor(mixed_r[:, :], change[:, :], V("cm_mix_r"), old, ALU.mult, ALU.add).then_inc(mixed_ready, 1)
                for f in range(NF):
                    dve.wait_ge(relu_ready, NF * b + f + 1 + NF)
                    nc.vector.tensor_tensor(hid[:, f, :], relu[:, f, :], relu[:, f, :], ALU.mult).then_inc(hid_ready, 1)
                ts = bass.ds(b * TPB, TPB)
                x1 = M.X1[:, ts, :].rearrange("p t d -> p (t d)")
                x = M.X[:, ts, :].rearrange("p t d -> p (t d)")
                nc.vector.tensor_tensor(x, x, x1, ALU.add)
                dve.wait_ge(down_ready, b + 1)
                dve.wait_ge(rr_ready, b + 1)
                nc.vector.tensor_tensor(res[:, :], down[:, :], rr[:, :], ALU.mult).then_inc(chain, 2)
                dve.wait_ge(chain, 2 * b + 2)
                nc.vector.tensor_tensor(x, x, res[:, :], ALU.add).then_inc(added, 1)


def rwkv_phase(nc, M, I):
    names = ("ln1_g", "ln1_b", "ln2_g", "ln2_b", "time_decay", "time_first", "cm_mix_k", "cm_mix_r",
             "tm_mix_k", "tm_mix_v", "tm_mix_r", "w")
    with Space(nc, "rw") as s:
        vec = s.sb("vec", [P, len(names)])

        def V(name):
            if name == "tm_mix":
                return vec[:, 8:11]
            return vec[:, names.index(name):names.index(name) + 1]

        with Space(nc, "rwl") as t:
            loaded = t.sem("loaded")
            block = t.block()

            @block.sync
            def _(sp):
                for name in names[:-1]:
                    sp.dma_start(V(name), I[name].rearrange("(p a) -> p a", a=1)).then_inc(loaded, 16)
                sp.wait_ge(loaded, 16 * (len(names) - 1))

        norm_phase(nc, M, "n1", M.X, 1e-5, eps2=1e-5, keep=M.X1, affine=(V("ln1_g"), V("ln1_b")))
        rwkv_mix_phase(nc, M, I, V)
        norm_phase(nc, M, "n2", M.X1, 1e-5, affine=(V("ln2_g"), V("ln2_b")))
        rwkv_channel_phase(nc, M, I, V)


def block_a(nc, M, I):
    with Space(nc, "xa") as s:
        M.X = s.sb("X", [P, NT, D])
        load_phase(nc, M, I, "load")
        norm_phase(nc, M, "na", M.X, 1e-5, eps2=1e-6, keep=M.X1)
    gdn_phase(nc, M, I)


def build(nc, I, out):
    with Space(nc, "m") as s:
        class M:
            X1 = s.sb("X1", [P, NT, D])
            HT = s.sb("HT", [P, B, 1 + S])
            ident = s.sb("ident", [P, P])
        block_a(nc, M, I)
        M.X = s.sb("X", [P, NT, D])
        load_phase(nc, M, I, "reload")
        norm_phase(nc, M, "nf", M.X1, 1e-6, rms=True)
        ffn_phase(nc, M, I, "ffa", I["W_fc"], I["W_proj"])
        norm_phase(nc, M, "nm", M.X, 1e-5)
        moe_phase(nc, M, I, "moe")
        rwkv_phase(nc, M, I)
        norm_phase(nc, M, "nm2", M.X, 1e-5)
        moe_phase(nc, M, I, "moe2")
        with Space(nc, "st") as t:
            stored = t.sem("stored")
            block = t.block()

            @block.sync
            def _(sp):
                sp.dma_start(out.rearrange("b (t p) d -> p (b t) d", p=P), M.X[:, :, :]).then_inc(stored, 16)
                sp.wait_ge(stored, 16)


def _constants():
    p = np.arange(P)
    same_expert = p[:, None] // B == p[None] // B
    masks = []
    for level in range(LEVELS):
        half = p >> level
        masks.append((half[:, None] // 2 == half[None] // 2) & (half[:, None] % 2 == 1) & (half[None] % 2 == 0))
    masks = np.stack(masks).astype(np.int32)
    bits = 1 << np.arange(BITS - 1, -1, -1)
    return {
        "ident": np.eye(P, dtype=np.float32),
        "group_ones": same_expert.astype(np.float32),
        "before_ones": (same_expert & (p[:, None] < p[None])).astype(np.float32),
        "bit_int": np.tile(bits.astype(np.int32), (P, 1)),
        "bit_val": np.tile(bits.astype(np.float32), (P, 1)),
        "mask_w": masks.transpose(1, 0, 2),
        "mask_t": masks.transpose(2, 0, 1),
    }


def kernel(**inputs):
    import concourse.bacc as bacc
    from concourse.bass_utils import run_bass_kernel_spmd

    given = {n: np.asarray(a) for n, a in inputs.items()}
    data = {"x": given["L0_attn_a_x"]}
    for n, a in given.items():
        if n.startswith("L0_attn_") and n != "L0_attn_a_x":
            data[n[len("L0_attn_a_"):]] = a
    data["A_log_rows"] = np.tile(data.pop("A_log"), P // H)[:, None]
    data["dt_bias_rows"] = np.tile(data.pop("dt_bias"), P // H)[:, None]
    data["Wg_moe"] = given["L0_ffn_Wg"]
    data["W1"] = given["L0_ffn_W1"]
    data["W2"] = given["L0_ffn_W2"]
    data["b1"] = given["L0_ffn_b1"].reshape(E, NF, P).transpose(2, 0, 1)
    data["b2"] = given["L0_ffn_b2"]
    data.update(_constants())
    nc = bacc.Bacc("TRN2", target_bir_lowering=False, num_devices=1)
    arrays, aps = {}, {}
    for n, a in data.items():
        arrays[f"in_{n}"] = np.ascontiguousarray(a)
        aps[n] = nc.dram_tensor(f"in_{n}", a.shape, mybir.dt.from_np(a.dtype), kind="ExternalInput").ap()
    out = nc.dram_tensor("out_x", (B, S, D), F32, kind="ExternalOutput").ap()
    build(nc, aps, out)
    r = run_bass_kernel_spmd(nc, [arrays], core_ids=[0])
    return r.results[0]["out_x"]
```
